# Optimizing a Trainium2 kernel written in Bass

```python
import numpy as np
import jax
import jax.numpy as jnp

def _softmax(x, axis=-1):
    return jax.nn.softmax(x, axis=axis)

def _gelu(x):
    return jax.nn.gelu(x, approximate=True)

def _silu(x):
    return jax.nn.silu(x)

def _sigmoid(x):
    return jax.nn.sigmoid(x)

def _layernorm(x, axis=-1, eps=1e-05):
    m = jnp.mean(x, axis=axis, keepdims=True)
    v = jnp.var(x, axis=axis, keepdims=True)
    return (x - m) / jnp.sqrt(v + eps)

def _scatter_add(tgt, idx, src, axis=0):
    return tgt.at[idx].add(src)

def _segment_sum(src, seg, n):
    return jax.ops.segment_sum(src, seg, n)
kernel_name = 'mk_macaron_d1_jaxref_r8_602ba0'

def setup_inputs(seed: int=0):
    np.random.seed(seed)
    _w = jnp.asarray

    def _L0_attn_setup():
        import jax, jax.numpy as jnp
        import numpy as np
        N_EMBD = 128
        N_HEAD = 16
        HEAD_DIM = N_EMBD // N_HEAD
        LATENT_DIM = N_EMBD // 2
        B, T = (4, 256)
        key = jax.random.key(seed)
        ks = jax.random.split(key, 5)

        def init(k, fan_in, fan_out):
            bound = 1.0 / np.sqrt(fan_in)
            return jax.random.uniform(k, (fan_in, fan_out), jnp.float32, -bound, bound)
        return {'x': jax.random.normal(ks[0], (B, T, N_EMBD), jnp.float32), 'Wc_down': init(ks[1], N_EMBD, LATENT_DIM), 'Wq_up': init(ks[2], LATENT_DIM, N_EMBD), 'Wkv_up': init(ks[3], LATENT_DIM, 2 * HEAD_DIM), 'Wc_proj': init(ks[4], N_EMBD, N_EMBD)}
    _L0_attn_in = _L0_attn_setup()

    def _L0_ffn_setup():
        import jax, jax.numpy as jnp
        import numpy as np
        B, N, D = (4, 256, 128)
        SPARSITY = 0.01
        key = jax.random.key(seed)
        k1, k2, k3 = jax.random.split(key, 3)
        x = jax.random.normal(k1, (B, N, D), dtype=jnp.float32)
        spatial = jax.random.normal(k2, (D, D), dtype=jnp.float32) * 0.02
        freq = jnp.fft.fft(spatial, axis=-1)
        k = int(D * SPARSITY)
        mag = jnp.abs(freq)
        kth = jax.lax.top_k(mag, k)[0][:, -1:]
        w_sparse = jnp.where(mag >= kth, freq, 0.0 + 0j)
        bias = jax.random.normal(k3, (D,), dtype=jnp.float32) * 0.01
        return {'x': x, 'w_freq_real': jnp.real(w_sparse).astype(jnp.float32), 'w_freq_imag': jnp.imag(w_sparse).astype(jnp.float32), 'bias': bias}
    _L0_ffn_in = _L0_ffn_setup()
    _d = {'L0_attn_x': _L0_attn_in['x'], 'L0_attn_Wc_down': _L0_attn_in['Wc_down'], 'L0_attn_Wq_up': _L0_attn_in['Wq_up'], 'L0_attn_Wkv_up': _L0_attn_in['Wkv_up'], 'L0_attn_Wc_proj': _L0_attn_in['Wc_proj'], 'L0_ffn_w_freq_real': _L0_ffn_in['w_freq_real'], 'L0_ffn_w_freq_imag': _L0_ffn_in['w_freq_imag'], 'L0_ffn_bias': _L0_ffn_in['bias']}
    _x0 = _d['L0_attn_x']
    _d['L0_attn_x'] = jax.random.normal(jax.random.fold_in(jax.random.key(seed), 1), (4, 1024, 128), dtype=_x0.dtype)
    del _x0
    return _d

def reference(L0_attn_x, L0_attn_Wc_down, L0_attn_Wq_up, L0_attn_Wkv_up, L0_attn_Wc_proj, L0_ffn_w_freq_real, L0_ffn_w_freq_imag, L0_ffn_bias):

    def _L0_attn_ref(x, Wc_down, Wq_up, Wkv_up, Wc_proj):
        import jax, jax.numpy as jnp
        import numpy as np
        N_EMBD = 128
        N_HEAD = 16
        HEAD_DIM = N_EMBD // N_HEAD
        LATENT_DIM = N_EMBD // 2
        B, T = (4, 256)
        Bsz, Tlen, C = x.shape
        latent = x @ Wc_down
        q = (latent @ Wq_up).reshape(Bsz, Tlen, N_HEAD, HEAD_DIM)
        kv = latent @ Wkv_up
        k, v = (kv[..., :HEAD_DIM], kv[..., HEAD_DIM:])
        scale = 1.0 / np.sqrt(HEAD_DIM)
        att = jnp.einsum('bthd,bsd->bhts', q, k) * scale
        causal = jnp.tril(jnp.ones((Tlen, Tlen), dtype=bool))
        att = jnp.where(causal[None, None], att, -jnp.inf)
        att = jax.nn.softmax(att, axis=-1)
        y = jnp.einsum('bhts,bsd->bthd', att, v).reshape(Bsz, Tlen, C)
        return y @ Wc_proj

    def _L0_ffn_ref(x, w_freq_real, w_freq_imag, bias):
        import jax, jax.numpy as jnp
        import numpy as np
        B, N, D = (4, 256, 128)
        SPARSITY = 0.01
        w = jax.lax.complex(w_freq_real, w_freq_imag)
        x_freq = jnp.fft.fft(x, axis=-1)
        y_freq = jnp.einsum('bnd,do->bno', x_freq, w)
        y = jnp.real(jnp.fft.ifft(y_freq, axis=-1))
        return y + bias
    x = L0_attn_x
    x = x + 0.5 * _L0_ffn_ref(_layernorm(x, axis=-1), L0_ffn_w_freq_real, L0_ffn_w_freq_imag, L0_ffn_bias)
    x = x + _L0_attn_ref(_layernorm(x, axis=-1), L0_attn_Wc_down, L0_attn_Wq_up, L0_attn_Wkv_up, L0_attn_Wc_proj)
    x = x + 0.5 * _L0_ffn_ref(_layernorm(x, axis=-1), L0_ffn_w_freq_real, L0_ffn_w_freq_imag, L0_ffn_bias)
    return x

_drawn_inputs = setup_inputs


def setup_inputs(seed=0):
    import zlib

    import numpy as np

    out = dict(_drawn_inputs(seed))
    spreads = {}
    factors = {'L0_attn_Wc_down': 4.031,
     'L0_attn_Wq_up': 8.0,
     'L0_attn_Wkv_up': 3.8,
     'L0_attn_Wc_proj': 3.942,
     'L0_ffn_bias': 6.128}
    for name, (base, spread) in spreads.items():
        noise = np.random.default_rng([zlib.crc32(name.encode()), seed]).standard_normal(out[name].shape)
        drawn = base * np.exp(spread * noise) if base else spread * noise
        out[name] = jnp.asarray(drawn.astype(out[name].dtype))
    for name, factor in factors.items():
        out[name] = (out[name] * factor).astype(out[name].dtype)
    return out
```

```python
from contextlib import ExitStack

import numpy as np

import concourse.bass as bass
from concourse import mybir

B, T, D = 4, 1024, 128
HEADS, HD, LATENT = 16, 8, 64
P = 128
BLK = 512
BLOCKS = B * T // BLK
TILES = BLK // P
GH = 4
GROUPS = HEADS // GH
UNITS = B * GROUPS
BODIES = UNITS // 2
PARTS = 3
ROWS = PARTS * PARTS * HD
QT = 32
NQT = T // QT
LEAD = 15
PRO_AHEAD, EPI_BEHIND = 3, 2
EPS = 1e-5
RSQRT_BITS = float(0x5F3759DF)
SCALE = 1.0 / float(np.sqrt(HD))
HIDE = -1e38
SELW = GH * (HD + 1)
C_ID, C_COS, C_SIN, C_NSIN, C_MASK, C_SEL = 0, 128, 256, 384, 512, 544
C_CAUSAL = C_SEL + SELW
C_ALL = C_CAUSAL + P


def constants():
    c = np.zeros((P, C_ALL), np.float64)
    j = np.arange(P)
    turn = 2 * np.pi * (np.outer(j, j) % P) / P
    c[:, C_ID:C_ID + P] = np.eye(P)
    c[:, C_COS:C_COS + P] = np.cos(turn)
    c[:, C_SIN:C_SIN + P] = np.sin(turn)
    c[:, C_NSIN:C_NSIN + P] = -np.sin(turn)
    q, s = np.meshgrid(np.arange(QT), np.arange(QT), indexing="ij")
    c[P - QT:, C_MASK:C_MASK + QT] = np.where(s > q, HIDE, 0.0)
    c[:, C_CAUSAL:] = np.where(j[:, None] > j[None, :], HIDE, 0.0)
    for h in range(GH):
        for d in range(HD + 1):
            c[32 * h + d, C_SEL + (HD + 1) * h + d] = 1.0
    return c.astype(np.float32)


def sweep1_tiles():
    out = []
    for tb in range(NQT):
        plain = QT * tb
        if tb < NQT // 2:
            out.append((tb, 0, 0, plain, True))
        else:
            out.append((tb, 0, 0, 512, False))
            out.append((tb, 1, 512, plain - 512, True))
    return out


S1 = sweep1_tiles()


def s1_cost(tile):
    return 67 + (tile[3] + QT * tile[4]) / 0.96


def groups_of(k):
    out = []
    for c in range(2):
        for i in range(4 * c + 4):
            first = max(0, P * i - 512 * c)
            out.append((k, c, i, 512 - first, first))
    return out


def body_schedule(pro, epi, s1_units):
    s1 = [(u, n) for u, lo, hi in s1_units for n in range(lo, hi)]
    done = {n: u for n, (u, t) in enumerate(s1) if t == len(S1) - 1}
    total = 2 * sum(s1_cost(t) for t in S1)
    groups = groups_of(0) + groups_of(1)
    work = sum(g[3] for g in groups)
    jobs = {7: ["sel00"], 13: ["sel01"], 18: ["sel10"]}
    pre = {}
    if pro:
        pre[2] = ["ln1"]
        for s, j in ((3, "zT"), (5, "ffn"), (8, "z2T"), (10, "q"), (12, "k"), (14, "v")):
            jobs.setdefault(s, []).append(j)
    if epi:
        for s, j in ((4, "yT"), (6, "proj"), (9, "z3T"), (11, "ffn3")):
            jobs.setdefault(s, []).append(j)
    out, at, spent, n_s1, n_st, last_job = [], 0, 0.0, 0, 0, None
    for s, g in enumerate(groups):
        k, c, i, w, first = g
        per = 1 if w > 256 else 2
        tiles = [(s, n_st + n, n * per, per) for n in range(GH // per)]
        n_st += len(tiles)
        at_end = at + w
        for n, t in enumerate(tiles):
            out.append(("st", g, t))
            upto = (at + w * (n + 1) / len(tiles)) / work * total
            while n_s1 < len(s1) and spent < upto:
                out.append(("s1", n_s1, s1[n_s1]))
                spent += s1_cost(S1[s1[n_s1][1]])
                if n_s1 in done:
                    out.append(("max", done[n_s1]))
                    jobs.setdefault(s + 1, []).append(f"mT{done[n_s1]}")
                n_s1 += 1
        at = at_end
        if s:
            out.append(("pv", s - 1, groups[s - 1]))
        for name in pre.get(s, []):
            out.append(("pre", name))
        for name in jobs.pop(s, []):
            if last_job:
                out.append(("post", last_job))
            out.append(("job", name))
            last_job = name
    rest = list(range(n_s1, len(s1)))
    for n in rest:
        out.append(("s1", n, s1[n]))
        assert n not in done
    out.append(("pv", len(groups) - 1, groups[-1]))
    for name in [j for s in sorted(jobs) for j in jobs[s]] + ["sel11"]:
        out += [("post", last_job), ("job", name)]
        last_job = name
    out.append(("post", last_job))
    return out


def macaron_program(nc, x, w_down, w_q, w_kv, w_proj, w_real, w_imag, bias, consts, out):
    f32, bf16 = mybir.dt.float32, mybir.dt.bfloat16
    i32 = mybir.dt.int32
    ALU, ACT, AX = mybir.AluOpType, mybir.ActivationFunctionType, mybir.AxisListType
    x_blk = x.rearrange("b (h n p) c -> (b h) p n c", n=TILES, p=P)
    out_blk = out.rearrange("b (h n p) c -> (b h) p n c", n=TILES, p=P)

    def dram(name, shape, dt):
        return nc.dram_tensor(name, shape, dt, kind="Internal").ap()

    q_dram = dram("q_parts_dram", [PARTS, B, P, T], bf16)
    q1_dram = dram("q_parts_by_32_rows_dram", [PARTS, B, GROUPS * HD, NQT, GH, QT], bf16)
    k_dram = dram("k_parts_dram", [B, PARTS, HD, T], bf16)
    v_dram = dram("v_dram", [B, P, T // P, 32], f32)
    x1_dram = dram("x1_dram", [BLOCKS, P, TILES * D], f32)
    y_dram = dram("y_dram", [B, T, D], f32)
    y_blk = y_dram.rearrange("b (h n p) c -> (b h) p n c", n=TILES, p=P)

    ctx = ExitStack()
    with ctx:
        def sb(name, shape, dt=f32):
            return ctx.enter_context(nc.sbuf_tensor(name, shape, dt))

        def bank(name):
            return ctx.enter_context(nc.psum_tensor(name, [P, 512], f32))

        def sem(name):
            return ctx.enter_context(nc.semaphore(name))

        const = sb("const", [P, C_ALL])
        ident, cos, sin, nsin = (const[:, c:c + P] for c in (C_ID, C_COS, C_SIN, C_NSIN))
        selector = const[:, C_SEL:C_SEL + SELW]
        ident16 = sb("ident16", [P, P], bf16)
        causal16 = sb("causal16", [P, P], bf16)
        wr, wi = sb("wr", [P, D]), sb("wi", [P, D])
        wd, wq, wkv = sb("wd", [P, LATENT]), sb("wq", [LATENT, D]), sb("wkv", [LATENT, 2 * HD])
        wp = sb("wp", [P, D])
        bias_half = sb("bias_half", [P, D])
        bias_in = sb("bias_in", [P, D])
        ab = sb("ab", [P, 2 * D])
        m_half = sb("m_half", [P, D])
        wdT = sb("wdT", [LATENT, P])
        w_dq, w_dk, w_dv = sb("w_dq", [P, D]), sb("w_dk", [P, HD]), sb("w_dv", [P, HD])
        q1 = sb("q1", [P, 2, NQT, GH * QT], bf16)
        q2 = sb("q2", [P, 2, GH, T], bf16)
        k_plain = sb("k_plain", [P, 2, T], bf16)
        k_corner = sb("k_corner", [P, 2, T], bf16)
        k2 = sb("k2", [P, 2, T], bf16)
        v1 = sb("v1", [P, 2, T // P, 32])
        probs = sb("probs", [P, 3, GH, 512])
        o_sb = sb("o_sb", [P, 512])
        rec = sb("rec", [P, TILES, GH])
        y_sb = sb("y_sb", [P, 2, T // P, GH * HD])
        mx = sb("mx", [P, 2, NQT])
        mx_pair = sb("mx_pair", [P, 2, NQT // 2, 2])
        m_rest = sb("m_rest", [P, NQT])
        m_parts = sb("m_parts", [P, PARTS, NQT], bf16)
        mT = sb("mT", [PARTS * NQT, P], bf16)
        x_sb, xb, x1, z1, z2 = (sb(n, [P, TILES, D]) for n in ("x_sb", "xb", "x1", "z1", "z2"))
        z1T, z2T = sb("z1T", [P, BLK]), sb("z2T", [P, BLK])
        q_parts, k_parts = sb("q_parts", [P, PARTS, BLK], bf16), sb("k_parts", [HD, PARTS, BLK], bf16)
        q_rest, k_rest = sb("q_rest", [P, BLK]), sb("k_rest", [HD, BLK])
        v_out = sb("v_out", [P, TILES, 32])
        y_in, x1_in, x2, x2b, z3, out_sb = (
            sb(n, [P, TILES, D]) for n in ("y_in", "x1_in", "x2", "x2b", "z3", "out_sb"))
        yT, z3T = sb("yT", [P, BLK]), sb("z3T", [P, BLK])
        stats, mv, rstd = sb("stats", [P, TILES, 6]), sb("mv", [P, TILES, 2]), sb("rstd", [P, TILES])
        var_eps, newton = sb("var_eps", [P, TILES]), sb("newton", [P, 2, TILES])
        guess_bits = sb("guess_bits", [P, TILES], i32)
        dve_dot, act_dot = sb("dve_dot", [1, 64]), sb("act_dot", [1, 2])
        st = [bank(f"st{n}") for n in range(3)]
        s1p = [bank(f"s1p{n}") for n in range(3)]
        o_ps = bank("o_ps")
        misc = bank("misc")
        m_bits = misc[:, 0:64].bitcast(bf16)

        (init_done, x1_ready, q_ready, k_ready, v_ready, pro_stored, out_ready, out_stored,
         y_ready, y_stored, mT_ready) = (sem(n) for n in (
             "init_done", "x1_ready", "q_ready", "k_ready", "v_ready", "pro_stored", "out_ready",
             "out_stored", "y_ready", "y_stored", "mT_ready"))
        w_loaded, prep_free, z_ready, misc_free, y_loaded, m_ready, s1_free = (sem(n) for n in (
            "w_loaded", "prep_free", "z_ready", "misc_free", "y_loaded", "m_ready", "s1_free"))
        s1_loaded = [sem(f"s1_loaded{n}") for n in range(2)]
        s2_loaded = [sem(f"s2_loaded{n}") for n in range(2)]
        exp_done, o_taken = sem("exp_done"), sem("o_taken")
        misc_act, st_ready, pv_done, act_start, act_chain = (sem(n) for n in (
            "misc_act", "st_ready", "pv_done", "act_start", "act_chain"))
        x_loaded, x1_loaded, misc_dve, s1_ready, xb_ready, x2b_ready, q1_ready, chain = (
            sem(n) for n in ("x_loaded", "x1_loaded", "misc_dve", "s1_ready", "xb_ready",
                             "x2b_ready", "q1_ready", "chain"))
        dve_start, pool_init = sem("dve_start"), sem("pool_init")
        x_seen, x2_seen, q2_ready, k2_ready = (sem(n) for n in (
            "x_seen", "x2_seen", "q2_ready", "k2_ready"))
        mv_ready, rstd_ready, pool_chain = sem("mv_ready"), sem("rstd_ready"), sem("pool_chain")

        block = ctx.enter_context(nc.Block())

        def counter():
            counts = {}

            def seen(s, n=1):
                key = s.name
                counts[key] = (s, counts.get(key, (s, 0))[1] + n)
                return counts[key][1]

            def settle(eng):
                for s, n in counts.values():
                    eng.sem_inc(s, -n)
                counts.clear()
            return seen, settle

        BODY_KINDS = [
            (0, 2, True, False, [(1, LEAD, 48), (2, 0, 48), (3, 0, LEAD)], 2),
            (2, 5, True, True, [(1, LEAD, 48), (2, 0, 48), (3, 0, LEAD)], 2),
            (5, 6, False, True, [(1, LEAD, 48), (2, 0, 48), (3, 0, LEAD)], 2),
            (6, 7, False, True, [(1, LEAD, 48), (2, 0, 48), (3, 0, LEAD)], 1),
            (7, 8, False, True, [(1, LEAD, 48)], 0),
        ]

        def run_bodies(eng, body):
            for first, end, pro, epi, s1_units, loads in BODY_KINDS:
                schedule = body_schedule(pro, epi, s1_units)
                if end - first > 1:
                    with eng.Fori(first, end) as i:
                        body(i, pro, epi, schedule, loads)
                else:
                    body(first, pro, epi, schedule, loads)

        PRE_S1 = [(0, n) for n in range(48)] + [(1, n) for n in range(LEAD)]

        @block.sync
        def _(sp):
            seen, settle = counter()
            for dst, src in ((const[:, :], consts), (wr[:, :], w_real), (wi[:, :], w_imag),
                             (wd[:, :], w_down), (wq[:, :], w_q), (wkv[:, :], w_kv),
                             (wp[:, :], w_proj)):
                sp.dma_start(dst, src).then_inc(w_loaded, 16)
            sp.dma_start(bias_in[:, :], bias.unsqueeze(0).broadcast_to([P, D])).then_inc(dve_start, 16)
            sp.dma_start(ab[:, 0:P], consts[:, C_ID:C_ID + P]).then_inc(dve_start, 16)
            sp.dma_start(ab[:, P:2 * P], consts[:, C_CAUSAL:C_ALL]).then_inc(dve_start, 16)
            sp.dma_start(x1_in[:, 0, 0:QT], consts[:, C_MASK:C_MASK + QT]).then_inc(act_start, 16)
            sp.dma_start(x1_in[:, 1, :], consts[:, C_ID:C_ID + P]).then_inc(act_start, 16)

            def load_x(j):
                sp.dma_start(x_sb[:, :, :], x_blk[bass.ds(j, 1)].rearrange("o p n c -> p (o n) c")
                             ).then_inc(x_loaded, 16)

            def store_x1(j):
                sp.wait_ge(x1_ready, seen(x1_ready))
                sp.dma_start(x1_dram[bass.ds(j, 1)].rearrange("o p f -> (o p) f"),
                             x1[:, :, :].rearrange("p n c -> p (n c)")).then_inc(pro_stored, 16)

            def store_q(j):
                sp.wait_ge(q_ready, seen(q_ready))
                sp.dma_start(q_dram[:, bass.ds(j // 2, 1), :, bass.ds((j % 2) * BLK, BLK)]
                             .rearrange("a o p t -> p (a o) t"), q_parts[:, :, :]).then_inc(pro_stored, 16)
                for a in range(PARTS):
                    for h in range(GH):
                        dst = q1_dram[a][bass.ds(j // 2, 1), :, bass.ds((j % 2) * (BLK // QT), BLK // QT), h, :]
                        sp.dma_start(dst.rearrange("o r n t -> (o r) n t"),
                                     q_parts[h::GH, a, :].rearrange("p (n t) -> p n t", t=QT)
                                     ).then_inc(pro_stored, 16)

            def store_k(j):
                sp.wait_ge(k_ready, seen(k_ready))
                sp.dma_start(k_dram[bass.ds(j // 2, 1), :, :, bass.ds((j % 2) * BLK, BLK)]
                             .rearrange("o a p t -> p (o a) t"), k_parts[:, :, :]).then_inc(pro_stored, 16)

            def store_v(j):
                sp.wait_ge(v_ready, seen(v_ready))
                sp.dma_start(v_dram[bass.ds(j // 2, 1), :, bass.ds((j % 2) * TILES, TILES), :]
                             .rearrange("o p n c -> (o p) n c"), v_out[:, :, :]).then_inc(pro_stored, 16)

            def load_q1(half, m):
                for a in range(PARTS):
                    src = q1_dram[a][bass.ds(half // 2, 1), bass.ds((half % 2) * 16 + HD * m, HD)]
                    sp.dma_start(
                        q1[24 * a:24 * a + 24, m, :, :].rearrange("p n f -> p (n f)"),
                        src.rearrange("o r n h t -> (o r) (n h t)").unsqueeze(0)
                        .broadcast_to([PARTS, HD, GH * T])).then_inc(s1_loaded[m], 16)

            def load_parts(dst, slot, half, m, done):
                for a in range(PARTS):
                    src = q_dram[a][bass.ds(half // 2, 1), bass.ds((half % 2) * 64 + 32 * m, 32), :]
                    sp.dma_start(
                        dst[24 * a:24 * a + 24, slot, :, :].rearrange("p h t -> p (h t)"),
                        src.rearrange("o (d h) t -> (o d) (h t)", h=GH).unsqueeze(0)
                        .broadcast_to([PARTS, HD, GH * T])).then_inc(done, 16)

            def load_k(dst, slot, half, done):
                sp.dma_start(dst[0:ROWS, slot, :],
                             k_dram[bass.ds(half // 2, 1)].rearrange("o c d t -> (o c d) t").unsqueeze(0)
                             .broadcast_to([PARTS, PARTS * HD, T])).then_inc(done, 16)

            def load_sweep1(half, m):
                load_q1(half, m)
                load_k(k_plain, m, half, s1_loaded[m])
                load_k(k_corner, m, half, s1_loaded[m])

            def load_sweep2(half, m):
                load_parts(q2, m, half, m, s2_loaded[m])
                load_k(k2, m, half, s2_loaded[m])
                sp.dma_start(v1[:, m, :, :].rearrange("p n c -> p (n c)"),
                             v_dram[bass.ds(half // 2, 1)].rearrange("o p n c -> (o p) (n c)")
                             ).then_inc(s2_loaded[m], 16)

            def max_rows(m):
                sp.wait_ge(mT_ready, seen(mT_ready))
                for h in range(GH):
                    sp.dma_start(
                        q2[ROWS:ROWS + PARTS, m, h, :].rearrange("a (n t) -> a n t", t=QT),
                        mT[:, QT * h:QT * h + QT]).then_inc(s2_loaded[m], 16)

            def store_y(half, m):
                sp.wait_ge(y_ready, seen(y_ready))
                sp.dma_start(
                    y_dram[bass.ds(half // 2, 1), :, bass.ds((half % 2) * 64 + 32 * m, 32)]
                    .rearrange("o (n p) c -> p (o n) c", p=P), y_sb[:, m, :, :]).then_inc(y_stored, 16)

            def load_epi(j):
                sp.dma_start(y_in[:, :, :], y_blk[bass.ds(j, 1)].rearrange("o p n c -> p (o n) c")
                             ).then_inc(y_loaded, 16)
                sp.dma_start(x1_in[:, :, :].rearrange("p n c -> p (n c)"),
                             x1_dram[bass.ds(j, 1)].rearrange("o p f -> (o p) f")).then_inc(x1_loaded, 16)

            def store_out(j):
                sp.wait_ge(out_ready, seen(out_ready))
                sp.dma_start(out_blk[bass.ds(j, 1)].rearrange("o p n c -> p (o n) c"), out_sb[:, :, :]
                             ).then_inc(out_stored, 16)
                sp.wait_ge(out_stored, seen(out_stored, 16))

            with sp.Fori(0, PRO_AHEAD) as j:
                load_x(j)
                store_x1(j)
                store_q(j)
                store_k(j)
                store_v(j)
                sp.wait_ge(pro_stored, seen(pro_stored, 256))
                settle(sp)
            sp.wait_ge(init_done, seen(init_done, 2))
            for m in range(2):
                load_sweep1(0, m)
                load_sweep2(0, m)
            max_rows(0)
            load_sweep1(1, 0)
            settle(sp)

            def body(i, pro, epi, schedule, loads):
                if epi:
                    load_epi(i - EPI_BEHIND)
                if pro:
                    load_x(i + PRO_AHEAD)
                max_rows(1)
                if loads >= 1:
                    load_sweep1(i + 1, 1)
                if pro:
                    store_x1(i + PRO_AHEAD)
                    store_q(i + PRO_AHEAD)
                if epi:
                    store_out(i - EPI_BEHIND)
                if pro:
                    store_k(i + PRO_AHEAD)
                store_y(i, 0)
                if loads >= 1:
                    load_sweep2(i + 1, 0)
                if pro:
                    store_v(i + PRO_AHEAD)
                    sp.wait_ge(pro_stored, seen(pro_stored, 256))
                sp.wait_ge(y_stored, seen(y_stored, 16))
                if loads >= 1:
                    max_rows(0)
                if loads >= 2:
                    load_sweep1(i + 2, 0)
                store_y(i, 1)
                if loads >= 1:
                    load_sweep2(i + 1, 1)
                sp.wait_ge(y_stored, seen(y_stored, 16))
                settle(sp)

            run_bodies(sp, body)
            with sp.Fori(BODIES - EPI_BEHIND, BLOCKS) as j:
                load_epi(j)
                store_out(j)
                settle(sp)

        @block.tensor
        def _(pe):
            seen, settle = counter()
            mm = nc.tensor.matmul
            pe.wait_ge(w_loaded, seen(w_loaded, 7 * 16))
            mm(misc[:, 0:P], wr[:, :], cos, start=True, stop=False)
            mm(misc[:, 0:P], wi[:, :], sin, start=False, stop=True)
            mm(misc[:, P:2 * P], wi[:, :], cos, start=True, stop=False)
            mm(misc[:, P:2 * P], wr[:, :], nsin, start=False, stop=True)
            nc.tensor.transpose(misc[0:LATENT, 2 * P:3 * P], wd[:, :], ident).then_inc(misc_dve, 1)
            pe.wait_ge(misc_free, seen(misc_free))
            mm(misc[:, 0:P], ab[:, 0:P], cos, start=True, stop=False)
            mm(misc[:, 0:P], ab[:, P:2 * P], nsin, start=False, stop=True)
            mm(misc[:, P:2 * P], wdT[:, :], wq[:, :], start=True, stop=True)
            mm(misc[:, 2 * P:2 * P + 2 * HD], wdT[:, :], wkv[:, :], start=True, stop=True
               ).then_inc(misc_dve, 1)
            pe.wait_ge(misc_free, seen(misc_free))

            def transposes(src, done):
                for n in range(TILES):
                    last = nc.tensor.transpose(misc[:, n * P:(n + 1) * P], src[:, n, :], ident)
                last.then_inc(done, 1)

            def by_tile(lhs, rhs, width, done):
                for n in range(TILES):
                    last = mm(misc[:, n * width:(n + 1) * width], lhs[:, n * P:(n + 1) * P], rhs,
                              start=True, stop=True)
                last.then_inc(done, 1)

            def job(name):
                if name == "zT" or name == "z2T" or name == "z3T":
                    pe.wait_ge(z_ready, seen(z_ready))
                    transposes({"zT": z1, "z2T": z2, "z3T": z3}[name], misc_act)
                elif name == "yT":
                    pe.wait_ge(y_loaded, seen(y_loaded, 16))
                    transposes(y_in, misc_act)
                elif name == "ffn":
                    by_tile(z1T, m_half[:, :], D, misc_dve)
                elif name == "ffn3":
                    by_tile(z3T, m_half[:, :], D, misc_dve)
                elif name == "proj":
                    by_tile(yT, wp[:, :], D, misc_dve)
                elif name == "q":
                    mm(misc[:, :], w_dq[:, :], z2T[:, :], start=True, stop=True).then_inc(misc_act, 1)
                elif name == "k":
                    mm(misc[0:HD, :], w_dk[:, :], z2T[:, :], start=True, stop=True).then_inc(misc_act, 1)
                elif name == "v":
                    by_tile(z2T, w_dv[:, :], HD, misc_act)
                elif name[:2] == "mT":
                    pe.wait_ge(m_ready, seen(m_ready))
                    nc.tensor.transpose(m_bits[0:PARTS * NQT, :],
                                        m_parts[:, :, :].rearrange("p a n -> p (a n)"), ident16[:, :]
                                        ).then_inc(misc_dve, 1)
                elif name[:3] == "sel":
                    pe.wait_ge(o_taken, seen(o_taken))
                    by_tile(o_sb, selector, SELW, misc_dve)

            def free(name):
                pe.wait_ge(misc_free, seen(misc_free))

            def sweep1(n, u, t):
                tb, piece, lo, plain, corner = S1[t]
                m = u % 2
                if t == 0:
                    pe.wait_ge(s1_loaded[m], seen(s1_loaded[m], 80))
                pe.wait_ge(s1_free, seen(s1_free))
                queries = q1[:, m, tb, :]
                ps = s1p[n % 3]
                if plain:
                    last = mm(ps[:, 0:plain], queries, k_plain[:, m, lo:lo + plain], start=True, stop=True)
                if corner:
                    last = mm(ps[:, plain:plain + QT], queries, k_corner[:, m, lo + plain:lo + plain + QT],
                              start=True, stop=True)
                last.then_inc(s1_ready, 1)

            settle(pe)
            with pe.Fori(0, PRO_AHEAD) as j:
                for name in ("zT", "ffn", "z2T", "q", "k", "v"):
                    job(name)
                    free(name)
                settle(pe)
            pe.sem_inc(s1_free, 3)
            for n, (u, t) in enumerate(PRE_S1):
                sweep1(n, u, t)
                if (u, t) == (0, 47):
                    job("mT0")
                    free("mT0")
            settle(pe)

            def body(i, pro, epi, schedule, loads):
                group_of = [item[2][0] for item in schedule if item[0] == "st"]
                exps = 0

                for item in schedule:
                    if item[0] == "st":
                        _, (k, c, ki, w, first), (s, n, h0, per) = item
                        if c == 0 and ki == 0 and h0 == 0:
                            pe.wait_ge(s2_loaded[k], seen(s2_loaded[k], 144))
                        if n - 2 > exps:
                            pe.wait_ge(exp_done, seen(exp_done, n - 2 - exps))
                            exps = n - 2
                        for e in range(per):
                            last = mm(st[n % 3][:, e * w:(e + 1) * w], k2[0:96, k, P * ki:P * ki + P],
                                      q2[0:96, k, h0 + e, 512 * c + first:512 * c + 512],
                                      start=True, stop=ki < 4 * c)
                            if ki >= 4 * c:
                                last = mm(st[n % 3][:, e * w:e * w + P], ident16[:, :], causal16[:, :],
                                          start=False, stop=True)
                        last.then_inc(st_ready, 1)
                    elif item[0] == "s1":
                        sweep1(item[1], *item[2])
                    elif item[0] == "pv":
                        _, s, (k, c, ki, w, first) = item
                        upto = sum(g <= s for g in group_of)
                        if upto > exps:
                            pe.wait_ge(exp_done, seen(exp_done, upto - exps))
                            exps = upto
                        for h in range(GH):
                            last = mm(o_ps[32 * h:32 * h + 32, first:512], v1[:, k, ki, :],
                                      probs[:, s % 3, h, 0:w], start=(ki == 0), stop=(ki == 4 * c + 3))
                        last.then_inc(pv_done, 1)
                    elif item[0] == "job":
                        job(item[1])
                    elif item[0] == "post":
                        free(item[1])
                settle(pe)

            run_bodies(pe, body)
            with pe.Fori(BODIES - EPI_BEHIND, BLOCKS) as j:
                for name in ("yT", "proj", "z3T", "ffn3"):
                    job(name)
                    free(name)
                settle(pe)

        @block.scalar
        def _(act):
            seen, settle = counter()
            copy = nc.scalar.copy
            act.wait_ge(act_start, seen(act_start, 32))
            for m in range(2):
                copy(q1[96:128, m, :, :].rearrange("p n (h t) -> p (n h) t", t=QT),
                     x1_in[96:128, 1, 96:128].unsqueeze(1).broadcast_to([32, GH * NQT, QT]))
                copy(k_corner[96:128, m, :].rearrange("p (n t) -> p n t", t=QT),
                     x1_in[96:128, 0, 0:QT].unsqueeze(1).broadcast_to([32, NQT, QT])
                     ).then_inc(act_chain, 1)
            act.wait_ge(act_chain, seen(act_chain, 2))
            copy(act_dot[:, 0:1], x1_in[0:1, 0, 0:1]).then_inc(init_done, 1)

            def post(name):
                if name in ("zT", "z2T", "z3T", "yT"):
                    act.wait_ge(misc_act, seen(misc_act))
                    dst = {"zT": z1T, "z2T": z2T, "z3T": z3T, "yT": yT}[name]
                    copy(dst[:, :], misc[:, :]).then_inc(misc_free, 1)
                elif name == "q":
                    act.wait_ge(misc_act, seen(misc_act))
                    copy(q_parts[:, 0, :], misc[:, :]).then_inc(q1_ready, 1)
                elif name == "k":
                    act.wait_ge(misc_act, seen(misc_act))
                    copy(k_parts[:, 0, :], misc[0:HD, :]).then_inc(q1_ready, 1)
                elif name == "v":
                    act.wait_ge(misc_act, seen(misc_act))
                    copy(v_out[:, :, 0:HD], misc[:, 0:TILES * HD].rearrange("p (n c) -> p n c", c=HD)
                         ).then_inc(misc_free, 1)
                    copy(act_dot[:, 1:2], act_dot[:, 0:1]).then_inc(v_ready, 1)

            settle(act)
            with act.Fori(0, PRO_AHEAD) as j:
                for name in ("zT", "z2T", "q", "k", "v"):
                    post(name)
                settle(act)
            act.sem_inc(pv_done, 3)

            def body(i, pro, epi, schedule, loads):
                for item in schedule:
                    if item[0] == "st":
                        _, (k, c, ki, w, first), (s, n, h0, per) = item
                        if h0 == 0:
                            act.wait_ge(pv_done, s + 1)
                        act.wait_ge(st_ready, seen(st_ready))
                        nc.scalar.activation(
                            probs[:, s % 3, h0:h0 + per, 0:w],
                            st[n % 3][:, 0:per * w].rearrange("p (e w) -> p e w", e=per),
                            ACT.Exp, scale=SCALE).then_inc(exp_done, 1)
                    elif item[0] == "pv":
                        _, s, (k, c, ki, w, first) = item
                        if ki == 4 * c + 3:
                            act.wait_ge(pv_done, s + 4)
                            copy(o_sb[:, :], o_ps[:, :]).then_inc(o_taken, 1)
                    elif item[0] == "post":
                        post(item[1])
                seen(pv_done, 24)
                settle(act)

            run_bodies(act, body)
            with act.Fori(BODIES - EPI_BEHIND, BLOCKS) as j:
                for name in ("yT", "z3T"):
                    post(name)
                settle(act)

        @block.vector
        def _(dve):
            seen, settle = counter()
            v = nc.vector

            def linked(ins):
                ins.then_inc(chain, 1)
                dve.wait_ge(chain, seen(chain))

            dots = [0]

            def dot(s):
                dots[0] = (dots[0] + 1) % 64
                v.memset(dve_dot[:, dots[0]:dots[0] + 1], 0.0).then_inc(s, 1)

            v.memset(q1[64:96, :, :, :], 0.0)
            v.memset(q2[64:96, :, :, :], 0.0)
            v.memset(k2[64:96, :, :], 1.0)
            v.memset(k_corner[64:96, :, :], 0.0)
            v.memset(v_out[:, :, :], 0.0)
            linked(v.memset(k_plain[64:128, :, :], 0.0))
            linked(v.memset(v_out[:, :, HD:HD + 1], 1.0))
            dot(init_done)
            dve.wait_ge(dve_start, seen(dve_start, 48))
            v.tensor_copy(ident16[:, :], ab[:, 0:P])
            v.tensor_copy(causal16[:, :], ab[:, P:2 * P])
            linked(v.tensor_scalar(bias_half[:, :], bias_in[:, :], 0.5, None, ALU.mult))
            dve.wait_ge(misc_dve, seen(misc_dve))
            v.tensor_copy(ab[:, :], misc[:, 0:2 * P])
            v.tensor_copy(wdT[:, :], misc[0:LATENT, 2 * P:3 * P]).then_inc(misc_free, 1)
            dve.wait_ge(misc_dve, seen(misc_dve))
            v.tensor_scalar(m_half[:, :], misc[:, 0:P], 0.5 / D, None, ALU.mult)
            v.tensor_copy(w_dq[:, :].rearrange("p (g d h) -> p g d h", g=GROUPS, d=HD),
                          misc[:, P:2 * P].rearrange("p (g h d) -> p g d h", g=GROUPS, d=HD))
            v.tensor_copy(w_dk[:, :], misc[:, 2 * P:2 * P + HD])
            v.tensor_copy(w_dv[:, :], misc[:, 2 * P + HD:2 * P + 2 * HD]).then_inc(misc_free, 1)

            def layernorm(src, dst, first_done, second_done):
                for n in range(TILES):
                    ins = v.bn_stats(stats[:, n, :], src[:, n, :])
                    if n == 0 and first_done is not None:
                        ins.then_inc(first_done, 1)
                    if n == 1 and second_done is not None:
                        ins.then_inc(second_done, 1)
                linked(ins)
                for n in range(TILES):
                    ins = v.bn_aggr(mv[:, n, :], stats[:, n, :])
                linked(ins)
                linked(v.tensor_scalar(var_eps[:, :], mv[:, :, 1], EPS, None, ALU.add))
                linked(v.tensor_scalar(guess_bits[:, :], var_eps[:, :].bitcast(i32), 1, None,
                                       ALU.logical_shift_right))
                v.tensor_scalar(rstd[:, :].bitcast(i32), guess_bits[:, :], -1.0, RSQRT_BITS,
                                ALU.mult, ALU.add).then_inc(mv_ready, 1)
                dve.wait_ge(rstd_ready, seen(rstd_ready))
                for n in range(TILES):
                    ins = v.tensor_scalar(dst[:, n, :], src[:, n, :], mv[:, n, 0:1], rstd[:, n:n + 1],
                                          ALU.subtract, ALU.mult)
                ins.then_inc(z_ready, 1)

            def flat(t):
                return t[:, :, :].rearrange("p n c -> p (n c)")

            def split_rest(ps, parts, rest, done):
                dve.wait_ge(q1_ready, seen(q1_ready))
                linked(v.tensor_tensor(rest[:, :], ps, parts[:, 0, :], ALU.subtract))
                v.tensor_copy(parts[:, 1, :], rest[:, :]).then_inc(done, 1)
                dot(misc_free)

            def pre(name):
                dve.wait_ge(x_loaded, seen(x_loaded, 16))
                layernorm(x_sb, z1, x_seen, None)

            def post(name):
                if name == "ffn":
                    dve.wait_ge(xb_ready, seen(xb_ready))
                    dve.wait_ge(misc_dve, seen(misc_dve))
                    linked(v.tensor_tensor(flat(x1), misc[:, :], flat(xb), ALU.add))
                    layernorm(x1, z2, misc_free, x1_ready)
                elif name == "q":
                    split_rest(misc[:, :], q_parts, q_rest, q2_ready)
                elif name == "k":
                    split_rest(misc[0:HD, :], k_parts, k_rest, k2_ready)
                elif name == "proj":
                    dve.wait_ge(x1_loaded, seen(x1_loaded, 16))
                    dve.wait_ge(misc_dve, seen(misc_dve))
                    linked(v.tensor_tensor(flat(x2), misc[:, :], flat(x1_in), ALU.add))
                    layernorm(x2, z3, misc_free, x2_seen)
                elif name == "ffn3":
                    dve.wait_ge(x2b_ready, seen(x2b_ready))
                    dve.wait_ge(misc_dve, seen(misc_dve))
                    v.tensor_tensor(flat(out_sb), misc[:, :], flat(x2b), ALU.add).then_inc(misc_free, 1)
                    dot(out_ready)
                elif name[:2] == "mT":
                    dve.wait_ge(misc_dve, seen(misc_dve))
                    v.tensor_copy(mT[:, :], m_bits[0:PARTS * NQT, :]).then_inc(misc_free, 1)
                    dot(mT_ready)
                elif name[:3] == "sel":
                    k, c = int(name[3]), int(name[4])
                    dve.wait_ge(misc_dve, seen(misc_dve))
                    sums = misc[:, 0:TILES * SELW].rearrange("p (n h e) -> p n h e", n=TILES, h=GH)
                    linked(v.reciprocal(rec[:, :, :], sums[:, :, :, HD]))
                    v.tensor_tensor(
                        y_sb[:, k, TILES * c:TILES * c + TILES, :].rearrange("p n (h d) -> p n h d", h=GH),
                        sums[:, :, :, 0:HD], rec[:, :, :].unsqueeze(3).broadcast_to([P, TILES, GH, HD]),
                        ALU.mult).then_inc(misc_free, 1)
                    if c == 1:
                        dot(y_ready)

            def sweep1_max(n, u, t):
                tb, piece, lo, plain, corner = S1[t]
                width = plain + QT * corner
                dst = mx[:, u % 2, tb:tb + 1] if tb < NQT // 2 else (
                    mx_pair[:, u % 2, tb - NQT // 2, piece:piece + 1])
                dve.wait_ge(s1_ready, seen(s1_ready))
                v.tensor_reduce(dst, s1p[n % 3][:, 0:width], axis=AX.X, op=ALU.max).then_inc(s1_free, 1)

            def max_parts(u):
                m = u % 2
                dot(chain)
                dve.wait_ge(chain, seen(chain))
                linked(v.tensor_tensor(mx[:, m, NQT // 2:], mx_pair[:, m, :, 0], mx_pair[:, m, :, 1],
                                       ALU.max))
                linked(v.tensor_scalar(m_parts[:, 0, :], mx[:, m, :], -1.0, None, ALU.mult))
                linked(v.scalar_tensor_tensor(m_rest[:, :], mx[:, m, :], -1.0, m_parts[:, 0, :],
                                              ALU.mult, ALU.subtract))
                linked(v.tensor_copy(m_parts[:, 1, :], m_rest[:, :]))
                v.tensor_tensor(m_parts[:, 2, :], m_rest[:, :], m_parts[:, 1, :], ALU.subtract
                                ).then_inc(m_ready, 1)

            settle(dve)
            with dve.Fori(0, PRO_AHEAD) as j:
                pre("ln1")
                for name in ("ffn", "q", "k"):
                    post(name)
                settle(dve)
            for n, (u, t) in enumerate(PRE_S1):
                sweep1_max(n, u, t)
                if (u, t) == (0, 47):
                    max_parts(0)
                    post("mT0")
            settle(dve)

            def body(i, pro, epi, schedule, loads):
                for item in schedule:
                    if item[0] == "s1":
                        sweep1_max(item[1], *item[2])
                    elif item[0] == "max":
                        max_parts(item[1])
                    elif item[0] == "pre":
                        pre(item[1])
                    elif item[0] == "post":
                        post(item[1])
                settle(dve)

            run_bodies(dve, body)
            with dve.Fori(BODIES - EPI_BEHIND, BLOCKS) as j:
                for name in ("proj", "ffn3"):
                    post(name)
                settle(dve)

        @block.gpsimd
        def _(pool):
            seen, settle = counter()
            g = nc.gpsimd

            def flat(t):
                return t[:, :, :].rearrange("p n c -> p (n c)")

            def with_bias(dst, src, ready):
                g.tensor_tensor(dst[:, :, :], src[:, :, :],
                                bias_half[:, :].unsqueeze(1).broadcast_to([P, TILES, D]), ALU.add
                                ).then_inc(ready, 1)

            def inverse_deviation():
                pool.wait_ge(mv_ready, seen(mv_ready))
                for n in range(3):
                    if n:
                        pool.wait_ge(pool_chain, seen(pool_chain))
                    g.tensor_tensor(newton[:, 0, :], rstd[:, :], rstd[:, :], ALU.mult).then_inc(pool_chain, 1)
                    pool.wait_ge(pool_chain, seen(pool_chain))
                    g.tensor_tensor(newton[:, 1, :], newton[:, 0, :], var_eps[:, :], ALU.mult
                                    ).then_inc(pool_chain, 1)
                    pool.wait_ge(pool_chain, seen(pool_chain))
                    g.tensor_scalar(newton[:, 0, :], newton[:, 1, :], -0.5, 1.5, ALU.mult, ALU.add
                                    ).then_inc(pool_chain, 1)
                    pool.wait_ge(pool_chain, seen(pool_chain))
                    g.tensor_tensor(rstd[:, :], rstd[:, :], newton[:, 0, :], ALU.mult
                                    ).then_inc(rstd_ready if n == 2 else pool_chain, 1)

            def pre(name):
                pool.wait_ge(x_seen, seen(x_seen))
                with_bias(xb, x_sb, xb_ready)
                inverse_deviation()

            def post(name):
                if name == "q":
                    pool.wait_ge(q2_ready, seen(q2_ready))
                    g.tensor_tensor(q_parts[:, 2, :], q_rest[:, :], q_parts[:, 1, :], ALU.subtract
                                    ).then_inc(q_ready, 1)
                elif name == "k":
                    pool.wait_ge(k2_ready, seen(k2_ready))
                    g.tensor_tensor(k_parts[:, 2, :], k_rest[:, :], k_parts[:, 1, :], ALU.subtract
                                    ).then_inc(k_ready, 1)
                elif name == "proj":
                    pool.wait_ge(x2_seen, seen(x2_seen))
                    with_bias(x2b, x2, x2b_ready)
                    inverse_deviation()
                elif name == "ffn":
                    inverse_deviation()

            with pool.Fori(0, PRO_AHEAD) as j:
                pre("ln1")
                for name in ("ffn", "q", "k"):
                    post(name)
                settle(pool)

            def body(i, pro, epi, schedule, loads):
                for item in schedule:
                    if item[0] == "pre":
                        pre(item[1])
                    elif item[0] == "post":
                        post(item[1])
                settle(pool)

            run_bodies(pool, body)
            with pool.Fori(BODIES - EPI_BEHIND, BLOCKS) as j:
                post("proj")
                settle(pool)


def kernel(L0_attn_x, L0_attn_Wc_down, L0_attn_Wq_up, L0_attn_Wkv_up, L0_attn_Wc_proj,
           L0_ffn_w_freq_real, L0_ffn_w_freq_imag, L0_ffn_bias):
    import concourse.bacc as bacc
    from concourse.bass_utils import run_bass_kernel_spmd

    nc = bacc.Bacc("TRN2", target_bir_lowering=False, num_devices=1)
    given = dict(x=L0_attn_x, w_down=L0_attn_Wc_down, w_q=L0_attn_Wq_up, w_kv=L0_attn_Wkv_up,
                 w_proj=L0_attn_Wc_proj, w_real=L0_ffn_w_freq_real, w_imag=L0_ffn_w_freq_imag,
                 bias=L0_ffn_bias, consts=constants())
    arrays, args = {}, []
    for name, a in given.items():
        a = np.ascontiguousarray(a)
        arrays[f"in_{name}"] = a
        args.append(nc.dram_tensor(f"in_{name}", a.shape, mybir.dt.from_np(a.dtype),
                                   kind="ExternalInput").ap())
    args.append(nc.dram_tensor("out", (B, T, D), mybir.dt.float32, kind="ExternalOutput").ap())
    macaron_program(nc, *args)
    r = run_bass_kernel_spmd(nc, [arrays], core_ids=[0])
    return r.results[0]["out"]
```

```python
from contextlib import ExitStack

import numpy as np

import concourse.bass as bass
from concourse import mybir

B, T, D = 4, 1024, 128
HEADS, HD, LATENT = 16, 8, 64
P = 128
BLK = 512
BLOCKS = B * T // BLK
TILES = BLK // P
GH = 4
GROUPS = HEADS // GH
UNITS = B * GROUPS
BODIES = UNITS // 2
PARTS = 3
ROWS = PARTS * PARTS * HD
QT = 32
NQT = T // QT
LEAD = 15
PRO_AHEAD, EPI_BEHIND = 3, 2
EPS = 1e-5
RSQRT_BITS = float(0x5F3759DF)
SCALE = 1.0 / float(np.sqrt(HD))
HIDE = -1e38
C_ID, C_COS, C_SIN, C_NSIN, C_CAUSAL, C_MASK = 0, 128, 256, 384, 512, 640
C_ALL = C_MASK + QT


def constants():
    c = np.zeros((P, C_ALL), np.float64)
    j = np.arange(P)
    turn = 2 * np.pi * (np.outer(j, j) % P) / P
    c[:, C_ID:C_ID + P] = np.eye(P)
    c[:, C_COS:C_COS + P] = np.cos(turn)
    c[:, C_SIN:C_SIN + P] = np.sin(turn)
    c[:, C_NSIN:C_NSIN + P] = -np.sin(turn)
    q, s = np.meshgrid(np.arange(QT), np.arange(QT), indexing="ij")
    c[P - QT:, C_MASK:C_MASK + QT] = np.where(s > q, HIDE, 0.0)
    c[:, C_CAUSAL:C_CAUSAL + P] = np.where(j[:, None] > j[None, :], HIDE, 0.0)
    return c.astype(np.float32)


def sweep1_tiles():
    out = []
    for tb in range(NQT):
        plain = QT * tb
        if tb < NQT // 2:
            out.append((tb, 0, 0, plain, True))
        else:
            out.append((tb, 0, 0, 512, False))
            out.append((tb, 1, 512, plain - 512, True))
    return out


S1 = sweep1_tiles()


def s1_cost(tile):
    return 67 + (tile[3] + QT * tile[4]) / 0.96


def groups_of(k):
    out = []
    for c in range(2):
        for i in range(4 * c + 4):
            first = max(0, P * i - 512 * c)
            out.append((k, c, i, 512 - first, first))
    return out


def body_schedule(pro, epi, s1_units):
    s1 = [(u, n) for u, lo, hi in s1_units for n in range(lo, hi)]
    done = {n: u for n, (u, t) in enumerate(s1) if t == len(S1) - 1}
    total = 2 * sum(s1_cost(t) for t in S1)
    groups = groups_of(0) + groups_of(1)
    work = sum(g[3] for g in groups)
    jobs = {7: ["sel00"], 14: ["sel01"], 18: ["sel10"]}
    other = {}
    if pro:
        other = {3: ["ln1a"], 5: ["ln1b"], 9: ["ln2b"]}
        for s, j in ((5, "zT"), (7, "ffn"), (9, "z2T"), (11, "q"), (13, "kv"), (16, "kT")):
            jobs.setdefault(s, []).append(j)
    if epi:
        other.setdefault(8, []).append("ln3b")
        for s, j in ((4, "yT"), (6, "proj"), (8, "z3T"), (10, "ffn3")):
            jobs.setdefault(s, []).append(j)
    out, at, spent, n_s1, n_st, last_job = [], 0, 0.0, 0, 0, None
    for s, g in enumerate(groups):
        k, c, i, w, first = g
        per = 1 if w > 256 else 2
        tiles = [(s, n_st + n, n * per, per) for n in range(GH // per)]
        n_st += len(tiles)
        for n, t in enumerate(tiles):
            out.append(("st", g, t))
            if n == 1 and last_job:
                out.append(("post", last_job))
                last_job = None
            upto = (at + w * (n + 1) / len(tiles)) / work * total
            while n_s1 < len(s1) and spent < upto:
                out.append(("s1", n_s1, s1[n_s1]))
                spent += s1_cost(S1[s1[n_s1][1]])
                if n_s1 in done:
                    out.append(("max", done[n_s1]))
                    jobs.setdefault(s + 1, []).append(f"mT{done[n_s1]}")
                n_s1 += 1
        at += w
        if s:
            out.append(("pv", s - 1, groups[s - 1]))
        for name in other.get(s, []):
            out.append(("do", name))
        for name in jobs.pop(s, []):
            if last_job:
                out.append(("post", last_job))
            out.append(("job", name))
            last_job = name
    if last_job:
        out.append(("post", last_job))
    for n in range(n_s1, len(s1)):
        out.append(("s1", n, s1[n]))
        assert n not in done
    out.append(("pv", len(groups) - 1, groups[-1]))
    for name in [j for s in sorted(jobs) for j in jobs[s]] + ["sel11"]:
        out += [("job", name), ("post", name)]
    return out


def macaron_program(nc, x, w_down, w_q, w_kv, w_proj, w_real, w_imag, bias, consts, out):
    f32, bf16 = mybir.dt.float32, mybir.dt.bfloat16
    i32 = mybir.dt.int32
    ALU, ACT, AX = mybir.AluOpType, mybir.ActivationFunctionType, mybir.AxisListType
    x_blk = x.rearrange("b (h n p) c -> (b h) p n c", n=TILES, p=P)
    out_blk = out.rearrange("b (h n p) c -> (b h) p n c", n=TILES, p=P)

    def dram(name, shape, dt):
        return nc.dram_tensor(name, shape, dt, kind="Internal").ap()

    q_dram = dram("q_parts_dram", [PARTS, B, GROUPS * HD, NQT, GH, QT], bf16)
    k_dram = dram("k_rows_dram", [B, PARTS, PARTS * HD, T], bf16)
    v_dram = dram("v_dram", [B, P, T // P, 32], f32)
    x1_dram = dram("x1_dram", [BLOCKS, P, TILES * D], f32)
    y_dram = dram("y_dram", [B, T, D], f32)
    y_blk = y_dram.rearrange("b (h n p) c -> (b h) p n c", n=TILES, p=P)

    ctx = ExitStack()
    with ctx:
        def sb(name, shape, dt=f32):
            return ctx.enter_context(nc.sbuf_tensor(name, shape, dt))

        def bank(name):
            return ctx.enter_context(nc.psum_tensor(name, [P, 512], f32))

        def sem(name):
            return ctx.enter_context(nc.semaphore(name))

        const = sb("const", [P, C_ALL])
        ident, cos, sin, nsin = (const[:, c:c + P] for c in (C_ID, C_COS, C_SIN, C_NSIN))
        ident16 = sb("ident16", [P, P], bf16)
        causal16 = sb("causal16", [P, P], bf16)
        wr, wi = sb("wr", [P, D]), sb("wi", [P, D])
        wd, wq, wkv = sb("wd", [P, LATENT]), sb("wq", [LATENT, D]), sb("wkv", [LATENT, 2 * HD])
        wp = sb("wp", [P, D])
        bias_half = sb("bias_half", [P, D])
        bias_in = sb("bias_in", [P, D])
        ab = sb("ab", [P, 2 * D])
        m_half = sb("m_half", [P, D])
        wdT = sb("wdT", [LATENT, P])
        w_dq, w_dkv = sb("w_dq", [P, D]), sb("w_dkv", [P, 2 * HD])
        q1 = sb("q1", [P, 2, NQT, GH * QT], bf16)
        q2 = sb("q2", [P, 2, NQT, GH * QT], bf16)
        k_plain = sb("k_plain", [P, 2, T], bf16)
        k_corner = sb("k_corner", [P, 2, T], bf16)
        k2 = sb("k2", [P, 2, T], bf16)
        v1 = sb("v1", [P, 2, T // P, 32])
        probs = sb("probs", [P, 3, GH, 512])
        o_sb = sb("o_sb", [P, 512])
        rec = sb("rec", [P, TILES, GH])
        y_sb = sb("y_sb", [P, 2, T // P, GH * HD])
        mx = sb("mx", [P, 2, NQT])
        mx_pair = sb("mx_pair", [P, 2, NQT // 2, 2])
        m_rest = sb("m_rest", [P, NQT])
        m_parts = sb("m_parts", [P, PARTS, NQT], bf16)
        mT = sb("mT", [PARTS * NQT, P], bf16)
        def twice(name, shape, dt=f32):
            return [sb(f"{name}{m}", shape, dt) for m in range(2)]

        x_sb, xb, x1, z1, z2 = (twice(n, [P, TILES, D]) for n in ("x_sb", "xb", "x1", "z1", "z2"))
        z1T, z2T = twice("z1T", [P, BLK]), twice("z2T", [P, BLK])
        q_parts, q_rest = twice("q_parts", [P, PARTS, BLK], bf16), twice("q_rest", [P, BLK])
        k_cols, k_rest = twice("k_cols", [P, TILES, PARTS, HD], bf16), twice("k_rest", [P, TILES, HD])
        k_parts = twice("k_parts", [PARTS * HD, BLK], bf16)
        v_out = twice("v_out", [P, TILES, 32])
        y_in, x1_in, x2, x2b, z3, out_sb = (
            twice(n, [P, TILES, D]) for n in ("y_in", "x1_in", "x2", "x2b", "z3", "out_sb"))
        yT, z3T = twice("yT", [P, BLK]), twice("z3T", [P, BLK])
        stats, mv, rstd, var_eps, guess_bits, newton = {}, {}, {}, {}, {}, {}
        for n in (1, 2, 3):
            for m in range(2):
                stats[n, m], mv[n, m] = sb(f"stats{n}{m}", [P, TILES, 6]), sb(f"mv{n}{m}", [P, TILES, 2])
                rstd[n, m], var_eps[n, m] = sb(f"rstd{n}{m}", [P, TILES]), sb(f"var_eps{n}{m}", [P, TILES])
                guess_bits[n, m] = sb(f"guess_bits{n}{m}", [P, TILES], i32)
                newton[n, m] = sb(f"newton{n}{m}", [P, 2, TILES])
        setup = sb("setup", [P, P + QT])
        dve_dot, act_dot = sb("dve_dot", [1, 64]), sb("act_dot", [1, 64])
        st = [bank(f"st{n}") for n in range(3)]
        s1p = [bank(f"s1p{n}") for n in range(3)]
        o_ps = bank("o_ps")
        misc = bank("misc")
        misc_of = [misc, o_ps]

        (init_done, x1_ready, q_ready, k_ready, v_ready, pro_stored, out_ready, out_stored,
         y_ready, y_stored, mT_ready) = (sem(n) for n in (
             "init_done", "x1_ready", "q_ready", "k_ready", "v_ready", "pro_stored", "out_ready",
             "out_stored", "y_ready", "y_stored", "mT_ready"))
        w_loaded, z_ready, m_ready, s1_free, kc_ready = (sem(n) for n in (
            "w_loaded", "z_ready", "m_ready", "s1_free", "kc_ready"))
        misc_free = [sem(f"misc_free{n}") for n in range(2)]
        s1_loaded = [sem(f"s1_loaded{n}") for n in range(2)]
        s2_loaded = [sem(f"s2_loaded{n}") for n in range(2)]
        exp_done, o_taken = sem("exp_done"), sem("o_taken")
        misc_act, st_ready, pv_done, act_start, act_chain = (sem(n) for n in (
            "misc_act", "st_ready", "pv_done", "act_start", "act_chain"))
        misc_dve, s1_ready, xb_ready, x2b_ready, q1_ready, chain = (
            sem(n) for n in ("misc_dve", "s1_ready", "xb_ready",
                             "x2b_ready", "q1_ready", "chain"))
        dve_start, pool_init = sem("dve_start"), sem("pool_init")
        x_loaded = [sem(f"x_loaded{n}") for n in range(2)]
        x1_loaded = [sem(f"x1_loaded{n}") for n in range(2)]
        y_loaded = [sem(f"y_loaded{n}") for n in range(2)]
        x_seen, x2_seen, q2_ready = (sem(n) for n in ("x_seen", "x2_seen", "q2_ready"))
        mv_ready, rstd_ready, pool_chain = sem("mv_ready"), sem("rstd_ready"), sem("pool_chain")

        block = ctx.enter_context(nc.Block())

        def counter():
            counts = {}

            def seen(s, n=1):
                key = s.name
                counts[key] = (s, counts.get(key, (s, 0))[1] + n)
                return counts[key][1]

            def settle(eng):
                for s, n in counts.values():
                    eng.sem_inc(s, -n)
                counts.clear()
            return seen, settle

        BODY_KINDS = [
            (0, 2, True, False, [(1, LEAD, 48), (2, 0, 48), (3, 0, LEAD)], 2),
            (2, 5, True, True, [(1, LEAD, 48), (2, 0, 48), (3, 0, LEAD)], 2),
            (5, 6, False, True, [(1, LEAD, 48), (2, 0, 48), (3, 0, LEAD)], 2),
            (6, 7, False, True, [(1, LEAD, 48), (2, 0, 48), (3, 0, LEAD)], 1),
            (7, 8, False, True, [(1, LEAD, 48)], 0),
        ]

        def run_bodies(eng, body):
            for first, end, pro, epi, s1_units, loads in BODY_KINDS:
                schedule = body_schedule(pro, epi, s1_units)
                if end - first > 1:
                    with eng.Fori(first, end) as i:
                        body(i, pro, epi, schedule, loads)
                else:
                    body(first, pro, epi, schedule, loads)

        def ahead_schedule():
            out = [("do", "ln1a")]
            todo = [("do", "ln1b")]
            for name in ("zT", "ffn", "ln2b", "z2T", "q", "kv", "kT"):
                todo += [("do", name)] if name == "ln2b" else [("job", name), ("post", name)]
            tiles = [(0, n) for n in range(48)] + [(1, n) for n in range(LEAD)]
            for n, (u, t) in enumerate(tiles):
                out.append(("s1", n, (u, t)))
                if n == 47:
                    out += [("max", 0)]
                if n == 52:
                    out += [("job", "mT0"), ("post", "mT0")]
                if n % 4 == 3 and todo:
                    out.append(todo.pop(0))
            return out + todo

        PRO_PAIR = ["ln1a", "ln1b", "zT", "ffn", "ln2b", "z2T", "q", "kv", "kT"]
        EPI_PAIR = ["yT", "proj", "ln3b", "z3T", "ffn3"]
        JOBS = {"zT", "ffn", "z2T", "q", "kv", "kT", "yT", "proj", "z3T", "ffn3"}

        @block.sync
        def _(sp):
            seen, settle = counter()
            for dst, src in ((const[:, :], consts), (wr[:, :], w_real), (wi[:, :], w_imag),
                             (wd[:, :], w_down), (wq[:, :], w_q), (wkv[:, :], w_kv),
                             (wp[:, :], w_proj)):
                sp.dma_start(dst, src).then_inc(w_loaded, 16)
            sp.dma_start(setup[:, 0:P], consts[:, C_ID:C_ID + P]).then_inc(act_start, 16)
            sp.dma_start(setup[:, P:], consts[:, C_MASK:C_MASK + QT]).then_inc(act_start, 16)
            sp.dma_start(bias_in[:, :], bias.unsqueeze(0).broadcast_to([P, D])).then_inc(dve_start, 16)
            sp.dma_start(ab[:, 0:P], consts[:, C_ID:C_ID + P]).then_inc(dve_start, 16)
            sp.dma_start(ab[:, P:2 * P], consts[:, C_CAUSAL:C_CAUSAL + P]).then_inc(dve_start, 16)

            def load_x(j, m=0):
                sp.dma_start(x_sb[m][:, :, :], x_blk[bass.ds(j, 1)].rearrange("o p n c -> p (o n) c")
                             ).then_inc(x_loaded[m], 16)

            def store_x1(j, m=0):
                sp.wait_ge(x1_ready, seen(x1_ready))
                sp.dma_start(x1_dram[bass.ds(j, 1)].rearrange("o p f -> (o p) f"),
                             x1[m][:, :, :].rearrange("p n c -> p (n c)")).then_inc(pro_stored, 16)

            def store_q(j, m=0):
                sp.wait_ge(q_ready, seen(q_ready))
                for a in range(PARTS):
                    for h in range(GH):
                        dst = q_dram[a][bass.ds(j // 2, 1), :, bass.ds((j % 2) * (BLK // QT), BLK // QT), h, :]
                        sp.dma_start(dst.rearrange("o r n t -> (o r) n t"),
                                     q_parts[m][h::GH, a, :].rearrange("p (n t) -> p n t", t=QT)
                                     ).then_inc(pro_stored, 16)

            def store_k(j, m=0):
                sp.wait_ge(k_ready, seen(k_ready))
                for a in range(PARTS):
                    sp.dma_start(k_dram[bass.ds(j // 2, 1), a, :, bass.ds((j % 2) * BLK, BLK)]
                                 .rearrange("o r t -> (o r) t"), k_parts[m][:, :]).then_inc(pro_stored, 16)

            def store_v(j, m=0):
                sp.wait_ge(v_ready, seen(v_ready))
                sp.dma_start(v_dram[bass.ds(j // 2, 1), :, bass.ds((j % 2) * TILES, TILES), :]
                             .rearrange("o p n c -> (o p) n c"), v_out[m][:, :, :]).then_inc(pro_stored, 16)

            def load_q(dst, half, m, done):
                for a in range(PARTS):
                    src = q_dram[a][bass.ds(half // 2, 1), bass.ds((half % 2) * 16 + HD * m, HD)]
                    sp.dma_start(
                        dst[24 * a:24 * a + 24, m, :, :].rearrange("p n f -> p (n f)"),
                        src.rearrange("o r n h t -> (o r) (n h t)").unsqueeze(0)
                        .broadcast_to([PARTS, HD, GH * T])).then_inc(done, 16)

            def load_k(dst, slot, half, done):
                sp.dma_start(dst[0:ROWS, slot, :],
                             k_dram[bass.ds(half // 2, 1)].rearrange("o a r t -> (o a r) t")
                             ).then_inc(done, 16)

            def load_sweep1(half, m):
                load_q(q1, half, m, s1_loaded[m])
                load_k(k_plain, m, half, s1_loaded[m])
                load_k(k_corner, m, half, s1_loaded[m])

            def load_sweep2(half, m):
                load_q(q2, half, m, s2_loaded[m])
                load_k(k2, m, half, s2_loaded[m])
                sp.dma_start(v1[:, m, :, :].rearrange("p n c -> p (n c)"),
                             v_dram[bass.ds(half // 2, 1)].rearrange("o p n c -> (o p) (n c)")
                             ).then_inc(s2_loaded[m], 16)

            def max_rows(m):
                sp.wait_ge(mT_ready, seen(mT_ready))
                sp.dma_start(q2[ROWS:ROWS + PARTS, m, :, :], mT[:, :]).then_inc(s2_loaded[m], 16)

            def store_y(half, m):
                sp.wait_ge(y_ready, seen(y_ready))
                sp.dma_start(
                    y_dram[bass.ds(half // 2, 1), :, bass.ds((half % 2) * 64 + 32 * m, 32)]
                    .rearrange("o (n p) c -> p (o n) c", p=P), y_sb[:, m, :, :]).then_inc(y_stored, 16)

            def load_epi(j, m=0):
                sp.dma_start(y_in[m][:, :, :], y_blk[bass.ds(j, 1)].rearrange("o p n c -> p (o n) c")
                             ).then_inc(y_loaded[m], 16)
                sp.dma_start(x1_in[m][:, :, :].rearrange("p n c -> p (n c)"),
                             x1_dram[bass.ds(j, 1)].rearrange("o p f -> (o p) f")).then_inc(x1_loaded[m], 16)

            def store_out(j, m=0):
                sp.wait_ge(out_ready, seen(out_ready))
                sp.dma_start(out_blk[bass.ds(j, 1)].rearrange("o p n c -> p (o n) c"), out_sb[m][:, :, :]
                             ).then_inc(out_stored, 16)

            for m in range(2):
                load_x(m, m)
            for store in (store_x1, store_q, store_v, store_k):
                for m in range(2):
                    store(m, m)
            load_x(2)
            sp.wait_ge(pro_stored, seen(pro_stored, 2 * 272))
            sp.wait_ge(init_done, seen(init_done, 2))
            load_sweep1(0, 0)
            load_sweep1(0, 1)
            load_sweep2(0, 0)
            load_sweep2(0, 1)
            store_x1(2)
            max_rows(0)
            load_sweep1(1, 0)
            store_q(2)
            store_v(2)
            store_k(2)
            sp.wait_ge(pro_stored, seen(pro_stored, 272))
            settle(sp)

            def body(i, pro, epi, schedule, loads):
                if epi:
                    load_epi(i - EPI_BEHIND)
                if pro:
                    load_x(i + PRO_AHEAD)
                max_rows(1)
                if loads >= 1:
                    load_sweep1(i + 1, 1)
                if pro:
                    store_x1(i + PRO_AHEAD)
                if epi:
                    store_out(i - EPI_BEHIND)
                if pro:
                    store_q(i + PRO_AHEAD)
                store_y(i, 0)
                if loads >= 1:
                    load_sweep2(i + 1, 0)
                if pro:
                    store_v(i + PRO_AHEAD)
                    store_k(i + PRO_AHEAD)
                sp.wait_ge(y_stored, seen(y_stored, 16))
                if loads >= 1:
                    max_rows(0)
                if pro:
                    sp.wait_ge(pro_stored, seen(pro_stored, 272))
                if loads >= 2:
                    load_sweep1(i + 2, 0)
                if epi:
                    sp.wait_ge(out_stored, seen(out_stored, 16))
                store_y(i, 1)
                if loads >= 1:
                    load_sweep2(i + 1, 1)
                sp.wait_ge(y_stored, seen(y_stored, 16))
                settle(sp)

            run_bodies(sp, body)
            for m in range(2):
                load_epi(BLOCKS - 2 + m, m)
            for m in range(2):
                store_out(BLOCKS - 2 + m, m)
            sp.wait_ge(out_stored, seen(out_stored, 32))

        @block.tensor
        def _(pe):
            seen, settle = counter()
            mm = nc.tensor.matmul
            pe.wait_ge(w_loaded, seen(w_loaded, 7 * 16))
            mm(misc[:, 0:P], wr[:, :], cos, start=True, stop=False)
            mm(misc[:, 0:P], wi[:, :], sin, start=False, stop=True)
            mm(misc[:, P:2 * P], wi[:, :], cos, start=True, stop=False)
            mm(misc[:, P:2 * P], wr[:, :], nsin, start=False, stop=True)
            nc.tensor.transpose(misc[0:LATENT, 2 * P:3 * P], wd[:, :], ident).then_inc(misc_dve, 1)
            pe.wait_ge(misc_free[0], seen(misc_free[0]))
            mm(misc[:, 0:P], ab[:, 0:P], cos, start=True, stop=False)
            mm(misc[:, 0:P], ab[:, P:2 * P], nsin, start=False, stop=True)
            mm(misc[:, P:2 * P], wdT[:, :], wq[:, :], start=True, stop=True)
            mm(misc[:, 2 * P:2 * P + 2 * HD], wdT[:, :], wkv[:, :], start=True, stop=True
               ).then_inc(misc_dve, 1)
            pe.wait_ge(misc_free[0], seen(misc_free[0]))
            settle(pe)

            def transposes(src, m, done):
                for n in range(TILES):
                    last = nc.tensor.transpose(misc_of[m][:, n * P:(n + 1) * P], src[:, n, :], ident)
                last.then_inc(done, 1)

            def by_tile(lhs, rhs, width, m, done):
                for n in range(TILES):
                    last = mm(misc_of[m][:, n * width:(n + 1) * width], lhs[:, n * P:(n + 1) * P], rhs,
                              start=True, stop=True)
                last.then_inc(done, 1)

            in_use = [False, False]

            def free(m=0):
                if in_use[m]:
                    pe.wait_ge(misc_free[m], seen(misc_free[m]))
                in_use[m] = False

            def job(name, m=0):
                free(m)
                in_use[m] = True
                if name in ("zT", "z2T", "z3T"):
                    pe.wait_ge(z_ready, seen(z_ready))
                    transposes({"zT": z1, "z2T": z2, "z3T": z3}[name][m], m, misc_act)
                elif name == "yT":
                    pe.wait_ge(y_loaded[m], seen(y_loaded[m], 16))
                    transposes(y_in[m], m, misc_act)
                elif name == "ffn":
                    by_tile(z1T[m], m_half[:, :], D, m, misc_dve)
                elif name == "ffn3":
                    by_tile(z3T[m], m_half[:, :], D, m, misc_dve)
                elif name == "proj":
                    by_tile(yT[m], wp[:, :], D, m, misc_dve)
                elif name == "q":
                    mm(misc_of[m][:, :], w_dq[:, :], z2T[m][:, :], start=True, stop=True
                       ).then_inc(misc_act, 1)
                elif name == "kv":
                    by_tile(z2T[m], w_dkv[:, :], 2 * HD, m, misc_act)
                elif name == "kT":
                    pe.wait_ge(kc_ready, seen(kc_ready))
                    for n in range(TILES):
                        last = nc.tensor.transpose(
                            misc_of[m][:, :].bitcast(bf16)[0:PARTS * HD, n * P:(n + 1) * P],
                            k_cols[m][:, n, :, :].rearrange("p a d -> p (a d)"), ident16[:, :])
                    last.then_inc(misc_act, 1)
                elif name[:2] == "mT":
                    pe.wait_ge(m_ready, seen(m_ready))
                    nc.tensor.transpose(misc[:, 0:64].bitcast(bf16)[0:PARTS * NQT, :],
                                        m_parts[:, :, :].rearrange("p a n -> p (a n)"), ident16[:, :]
                                        ).then_inc(misc_dve, 1)
                elif name[:3] == "sel":
                    pe.wait_ge(o_taken, seen(o_taken))
                    for n in range(TILES):
                        last = nc.tensor.transpose(misc[:, n * P:(n + 1) * P],
                                                   o_sb[:, n * P:(n + 1) * P], ident)
                    last.then_inc(misc_dve, 1)

            def sweep1(n, u, t):
                tb, piece, lo, plain, corner = S1[t]
                m = u % 2
                if t == 0:
                    pe.wait_ge(s1_loaded[m], seen(s1_loaded[m], 80))
                pe.wait_ge(s1_free, seen(s1_free))
                queries = q1[:, m, tb, :]
                ps = s1p[n % 3]
                if plain:
                    last = mm(ps[:, 0:plain], queries, k_plain[:, m, lo:lo + plain], start=True, stop=True)
                if corner:
                    last = mm(ps[:, plain:plain + QT], queries, k_corner[:, m, lo + plain:lo + plain + QT],
                              start=True, stop=True)
                last.then_inc(s1_ready, 1)

            def in_pairs(names):
                for name in names:
                    for m in range(2):
                        if name in JOBS:
                            job(name, m)
                free(0)
                free(1)
                settle(pe)

            in_pairs(PRO_PAIR)
            pe.sem_inc(s1_free, 3)
            for item in ahead_schedule():
                if item[0] == "s1":
                    sweep1(item[1], *item[2])
                elif item[0] == "job":
                    job(item[1])
            free()
            settle(pe)

            def body(i, pro, epi, schedule, loads):
                group_of = [item[2][0] for item in schedule if item[0] == "st"]
                exps = 0

                for item in schedule:
                    if item[0] == "st":
                        _, (k, c, ki, w, first), (s, n, h0, per) = item
                        if c == 0 and ki == 0 and h0 == 0:
                            pe.wait_ge(s2_loaded[k], seen(s2_loaded[k], 96))
                        if n - 2 > exps:
                            pe.wait_ge(exp_done, seen(exp_done, n - 2 - exps))
                            exps = n - 2
                        for e in range(per):
                            last = mm(st[n % 3][:, e * w:(e + 1) * w], k2[0:96, k, P * ki:P * ki + P],
                                      q2[0:96, k, 16 * c + first // QT:16 * c + 16,
                                         QT * (h0 + e):QT * (h0 + e + 1)],
                                      start=True, stop=ki < 4 * c)
                            if ki >= 4 * c:
                                last = mm(st[n % 3][:, e * w:e * w + P], ident16[:, :], causal16[:, :],
                                          start=False, stop=True)
                        last.then_inc(st_ready, 1)
                    elif item[0] == "s1":
                        sweep1(item[1], *item[2])
                    elif item[0] == "pv":
                        _, s, (k, c, ki, w, first) = item
                        upto = sum(g <= s for g in group_of)
                        if upto > exps:
                            pe.wait_ge(exp_done, seen(exp_done, upto - exps))
                            exps = upto
                        for h in range(GH):
                            last = mm(o_ps[32 * h:32 * h + 32, first:512], v1[:, k, ki, :],
                                      probs[:, s % 3, h, 0:w], start=(ki == 0), stop=(ki == 4 * c + 3))
                        last.then_inc(pv_done, 1)
                    elif item[0] == "job":
                        job(item[1])
                free()
                settle(pe)

            run_bodies(pe, body)
            in_pairs(EPI_PAIR)

        @block.scalar
        def _(act):
            seen, settle = counter()
            copy = nc.scalar.copy
            act.wait_ge(act_start, seen(act_start, 32))
            for m in range(2):
                copy(q1[96:128, m, :, :].rearrange("p n (h t) -> p (n h) t", t=QT),
                     setup[96:128, 96:128].unsqueeze(1).broadcast_to([32, GH * NQT, QT]))
                copy(k_corner[96:128, m, :].rearrange("p (n t) -> p n t", t=QT),
                     setup[96:128, P:P + QT].unsqueeze(1).broadcast_to([32, NQT, QT])
                     ).then_inc(act_chain, 1)
            act.wait_ge(act_chain, seen(act_chain, 2))
            dots = [0]

            def dot(s):
                dots[0] = (dots[0] + 1) % 64
                copy(act_dot[:, dots[0]:dots[0] + 1], setup[0:1, 0:1]).then_inc(s, 1)

            dot(init_done)

            def post(name, m=0):
                bank_ = misc_of[m]
                if name in ("zT", "z2T", "z3T", "yT"):
                    act.wait_ge(misc_act, seen(misc_act))
                    dst = {"zT": z1T, "z2T": z2T, "z3T": z3T, "yT": yT}[name][m]
                    copy(dst[:, :], bank_[:, :]).then_inc(misc_free[m], 1)
                elif name == "q":
                    act.wait_ge(misc_act, seen(misc_act))
                    copy(q_parts[m][:, 0, :], bank_[:, :]).then_inc(q1_ready, 1)
                elif name == "kv":
                    act.wait_ge(misc_act, seen(misc_act))
                    copy(v_out[m][:, :, 0:HD],
                         bank_[:, 0:TILES * 2 * HD].rearrange("p (n c) -> p n c", c=2 * HD)[:, :, HD:]
                         ).then_inc(q1_ready, 1)
                    dot(v_ready)
                elif name == "kT":
                    act.wait_ge(misc_act, seen(misc_act))
                    copy(k_parts[m][:, :], bank_[:, :].bitcast(bf16)[0:PARTS * HD, 0:BLK]
                         ).then_inc(misc_free[m], 1)
                    dot(k_ready)

            for name in PRO_PAIR:
                for m in range(2):
                    post(name, m)
            for item in ahead_schedule():
                if item[0] == "post":
                    post(item[1])
            settle(act)
            act.sem_inc(pv_done, 3)

            def body(i, pro, epi, schedule, loads):
                for item in schedule:
                    if item[0] == "st":
                        _, (k, c, ki, w, first), (s, n, h0, per) = item
                        if h0 == 0:
                            act.wait_ge(pv_done, s + 1)
                        act.wait_ge(st_ready, seen(st_ready))
                        nc.scalar.activation(
                            probs[:, s % 3, h0:h0 + per, 0:w],
                            st[n % 3][:, 0:per * w].rearrange("p (e w) -> p e w", e=per),
                            ACT.Exp, scale=SCALE).then_inc(exp_done, 1)
                    elif item[0] == "pv":
                        _, s, (k, c, ki, w, first) = item
                        if ki == 4 * c + 3:
                            act.wait_ge(pv_done, s + 4)
                            copy(o_sb[:, :], o_ps[:, :]).then_inc(o_taken, 1)
                    elif item[0] == "post":
                        post(item[1])
                seen(pv_done, 24)
                settle(act)

            run_bodies(act, body)
            for name in EPI_PAIR:
                for m in range(2):
                    post(name, m)

        @block.vector
        def _(dve):
            seen, settle = counter()
            v = nc.vector

            def linked(ins):
                ins.then_inc(chain, 1)
                dve.wait_ge(chain, seen(chain))

            dots = [0]

            def dot(s):
                dots[0] = (dots[0] + 1) % 64
                v.memset(dve_dot[:, dots[0]:dots[0] + 1], 0.0).then_inc(s, 1)

            v.memset(q1[64:96, :, :, :], 0.0)
            v.memset(q2[64:96, :, :, :], 0.0)
            v.memset(k2[64:96, :, :], 1.0)
            v.memset(k_corner[64:96, :, :], 0.0)
            v.memset(v_out[0][:, :, :], 0.0)
            v.memset(v_out[1][:, :, :], 0.0)
            linked(v.memset(k_plain[64:128, :, :], 0.0))
            v.memset(v_out[0][:, :, HD:HD + 1], 1.0)
            linked(v.memset(v_out[1][:, :, HD:HD + 1], 1.0))
            dot(init_done)
            dve.wait_ge(dve_start, seen(dve_start, 48))
            v.tensor_copy(ident16[:, :], ab[:, 0:P])
            v.tensor_copy(causal16[:, :], ab[:, P:2 * P])
            linked(v.tensor_scalar(bias_half[:, :], bias_in[:, :], 0.5, None, ALU.mult))
            dve.wait_ge(misc_dve, seen(misc_dve))
            v.tensor_copy(ab[:, :], misc[:, 0:2 * P])
            v.tensor_copy(wdT[:, :], misc[0:LATENT, 2 * P:3 * P]).then_inc(misc_free[0], 1)
            dve.wait_ge(misc_dve, seen(misc_dve))
            v.tensor_scalar(m_half[:, :], misc[:, 0:P], 0.5 / D, None, ALU.mult)
            v.tensor_copy(w_dq[:, :].rearrange("p (g d h) -> p g d h", g=GROUPS, d=HD),
                          misc[:, P:2 * P].rearrange("p (g h d) -> p g d h", g=GROUPS, d=HD))
            v.tensor_copy(w_dkv[:, :], misc[:, 2 * P:2 * P + 2 * HD]).then_inc(misc_free[0], 1)

            def statistics(src, ln, first_done, second_done):
                for n in range(TILES):
                    ins = v.bn_stats(stats[ln][:, n, :], src[:, n, :])
                    if n == 0 and first_done is not None:
                        ins.then_inc(first_done, 1)
                    if n == 1 and second_done is not None:
                        ins.then_inc(second_done, 1)
                linked(ins)
                for n in range(TILES):
                    ins = v.bn_aggr(mv[ln][:, n, :], stats[ln][:, n, :])
                linked(ins)
                linked(v.tensor_scalar(var_eps[ln][:, :], mv[ln][:, :, 1], EPS, None, ALU.add))
                linked(v.tensor_scalar(guess_bits[ln][:, :], var_eps[ln][:, :].bitcast(i32), 1, None,
                                       ALU.logical_shift_right))
                v.tensor_scalar(rstd[ln][:, :].bitcast(i32), guess_bits[ln][:, :], -1.0, RSQRT_BITS,
                                ALU.mult, ALU.add).then_inc(mv_ready, 1)

            def normalise(src, dst, ln):
                dve.wait_ge(rstd_ready, seen(rstd_ready))
                for n in range(TILES):
                    ins = v.tensor_scalar(dst[:, n, :], src[:, n, :], mv[ln][:, n, 0:1],
                                          rstd[ln][:, n:n + 1], ALU.subtract, ALU.mult)
                ins.then_inc(z_ready, 1)

            def flat(t):
                return t[:, :, :].rearrange("p n c -> p (n c)")

            def do(name, m=0):
                if name == "ln1a":
                    dve.wait_ge(x_loaded[m], seen(x_loaded[m], 16))
                    statistics(x_sb[m], (1, m), x_seen, None)
                elif name == "ln1b":
                    normalise(x_sb[m], z1[m], (1, m))
                elif name == "ln2b":
                    normalise(x1[m], z2[m], (2, m))
                elif name == "ln3b":
                    normalise(x2[m], z3[m], (3, m))

            def post(name, m=0):
                bank_ = misc_of[m]
                if name == "ffn":
                    dve.wait_ge(xb_ready, seen(xb_ready))
                    dve.wait_ge(misc_dve, seen(misc_dve))
                    linked(v.tensor_tensor(flat(x1[m]), bank_[:, :], flat(xb[m]), ALU.add))
                    statistics(x1[m], (2, m), misc_free[m], x1_ready)
                elif name == "q":
                    dve.wait_ge(q1_ready, seen(q1_ready))
                    linked(v.tensor_tensor(q_rest[m][:, :], bank_[:, :], q_parts[m][:, 0, :], ALU.subtract))
                    v.tensor_copy(q_parts[m][:, 1, :], q_rest[m][:, :]).then_inc(q2_ready, 1)
                    dot(misc_free[m])
                elif name == "kv":
                    dve.wait_ge(q1_ready, seen(q1_ready))
                    k_ps = bank_[:, 0:TILES * 2 * HD].rearrange("p (n c) -> p n c", c=2 * HD)[:, :, 0:HD]
                    linked(v.tensor_copy(k_cols[m][:, :, 0, :], k_ps))
                    linked(v.tensor_tensor(k_rest[m][:, :, :], k_ps, k_cols[m][:, :, 0, :], ALU.subtract))
                    dot(misc_free[m])
                    linked(v.tensor_copy(k_cols[m][:, :, 1, :], k_rest[m][:, :, :]))
                    v.tensor_tensor(k_cols[m][:, :, 2, :], k_rest[m][:, :, :], k_cols[m][:, :, 1, :],
                                    ALU.subtract).then_inc(kc_ready, 1)
                elif name == "proj":
                    dve.wait_ge(x1_loaded[m], seen(x1_loaded[m], 16))
                    dve.wait_ge(misc_dve, seen(misc_dve))
                    linked(v.tensor_tensor(flat(x2[m]), bank_[:, :], flat(x1_in[m]), ALU.add))
                    statistics(x2[m], (3, m), misc_free[m], x2_seen)
                elif name == "ffn3":
                    dve.wait_ge(x2b_ready, seen(x2b_ready))
                    dve.wait_ge(misc_dve, seen(misc_dve))
                    v.tensor_tensor(flat(out_sb[m]), bank_[:, :], flat(x2b[m]), ALU.add
                                    ).then_inc(misc_free[m], 1)
                    dot(out_ready)
                elif name[:2] == "mT":
                    dve.wait_ge(misc_dve, seen(misc_dve))
                    v.tensor_copy(mT[:, :], misc[:, 0:64].bitcast(bf16)[0:PARTS * NQT, :]
                                  ).then_inc(misc_free[m], 1)
                    dot(mT_ready)
                elif name[:3] == "sel":
                    k, c = int(name[3]), int(name[4])
                    dve.wait_ge(misc_dve, seen(misc_dve))
                    sums = misc[:, :].rearrange("p (n h e) -> p n h e", n=TILES, h=GH)
                    linked(v.reciprocal(rec[:, :, :], sums[:, :, :, HD]))
                    v.tensor_tensor(
                        y_sb[:, k, TILES * c:TILES * c + TILES, :].rearrange("p n (h d) -> p n h d", h=GH),
                        sums[:, :, :, 0:HD], rec[:, :, :].unsqueeze(3).broadcast_to([P, TILES, GH, HD]),
                        ALU.mult).then_inc(misc_free[m], 1)
                    if c == 1:
                        dot(y_ready)

            def sweep1_max(n, u, t):
                tb, piece, lo, plain, corner = S1[t]
                width = plain + QT * corner
                dst = mx[:, u % 2, tb:tb + 1] if tb < NQT // 2 else (
                    mx_pair[:, u % 2, tb - NQT // 2, piece:piece + 1])
                dve.wait_ge(s1_ready, seen(s1_ready))
                v.tensor_reduce(dst, s1p[n % 3][:, 0:width], axis=AX.X, op=ALU.max).then_inc(s1_free, 1)

            def max_parts(u):
                m = u % 2
                dot(chain)
                dve.wait_ge(chain, seen(chain))
                linked(v.tensor_tensor(mx[:, m, NQT // 2:], mx_pair[:, m, :, 0], mx_pair[:, m, :, 1],
                                       ALU.max))
                linked(v.tensor_scalar(m_parts[:, 0, :], mx[:, m, :], -1.0, None, ALU.mult))
                linked(v.scalar_tensor_tensor(m_rest[:, :], mx[:, m, :], -1.0, m_parts[:, 0, :],
                                              ALU.mult, ALU.subtract))
                linked(v.tensor_copy(m_parts[:, 1, :], m_rest[:, :]))
                v.tensor_tensor(m_parts[:, 2, :], m_rest[:, :], m_parts[:, 1, :], ALU.subtract
                                ).then_inc(m_ready, 1)

            def take(item):
                if item[0] == "s1":
                    sweep1_max(item[1], *item[2])
                elif item[0] == "max":
                    max_parts(item[1])
                elif item[0] == "do":
                    do(item[1])
                elif item[0] == "post":
                    post(item[1])

            for name in PRO_PAIR:
                for m in range(2):
                    do(name, m)
                    post(name, m)
            for item in ahead_schedule():
                take(item)
            settle(dve)

            def body(i, pro, epi, schedule, loads):
                for item in schedule:
                    take(item)
                settle(dve)

            run_bodies(dve, body)
            for name in EPI_PAIR:
                for m in range(2):
                    do(name, m)
                    post(name, m)

        @block.gpsimd
        def _(pool):
            seen, settle = counter()
            g = nc.gpsimd

            def flat(t):
                return t[:, :, :].rearrange("p n c -> p (n c)")

            def with_bias(dst, src, ready):
                g.tensor_tensor(dst[:, :, :], src[:, :, :],
                                bias_half[:, :].unsqueeze(1).broadcast_to([P, TILES, D]), ALU.add
                                ).then_inc(ready, 1)

            def inverse_deviation(ln):
                pool.wait_ge(mv_ready, seen(mv_ready))
                a, b = newton[ln][:, 0, :], newton[ln][:, 1, :]
                for n in range(3):
                    if n:
                        pool.wait_ge(pool_chain, seen(pool_chain))
                    g.tensor_tensor(a, rstd[ln][:, :], rstd[ln][:, :], ALU.mult).then_inc(pool_chain, 1)
                    pool.wait_ge(pool_chain, seen(pool_chain))
                    g.tensor_tensor(b, a, var_eps[ln][:, :], ALU.mult).then_inc(pool_chain, 1)
                    pool.wait_ge(pool_chain, seen(pool_chain))
                    g.tensor_scalar(a, b, -0.5, 1.5, ALU.mult, ALU.add).then_inc(pool_chain, 1)
                    pool.wait_ge(pool_chain, seen(pool_chain))
                    g.tensor_tensor(rstd[ln][:, :], rstd[ln][:, :], a, ALU.mult
                                    ).then_inc(rstd_ready if n == 2 else pool_chain, 1)

            def work(name, m=0):
                if name == "ln1a":
                    inverse_deviation((1, m))
                    pool.wait_ge(x_seen, seen(x_seen))
                    with_bias(xb[m], x_sb[m], xb_ready)
                elif name == "ffn":
                    inverse_deviation((2, m))
                elif name == "q":
                    pool.wait_ge(q2_ready, seen(q2_ready))
                    g.tensor_tensor(q_parts[m][:, 2, :], q_rest[m][:, :], q_parts[m][:, 1, :], ALU.subtract
                                    ).then_inc(q_ready, 1)
                elif name == "proj":
                    inverse_deviation((3, m))
                    pool.wait_ge(x2_seen, seen(x2_seen))
                    with_bias(x2b[m], x2[m], x2b_ready)

            for name in PRO_PAIR:
                for m in range(2):
                    work(name, m)
            for item in ahead_schedule():
                if item[0] in ("do", "post"):
                    work(item[1])
            settle(pool)

            def body(i, pro, epi, schedule, loads):
                for item in schedule:
                    if item[0] in ("do", "post"):
                        work(item[1])
                settle(pool)

            run_bodies(pool, body)
            for name in EPI_PAIR:
                for m in range(2):
                    work(name, m)


def kernel(L0_attn_x, L0_attn_Wc_down, L0_attn_Wq_up, L0_attn_Wkv_up, L0_attn_Wc_proj,
           L0_ffn_w_freq_real, L0_ffn_w_freq_imag, L0_ffn_bias):
    import concourse.bacc as bacc
    from concourse.bass_utils import run_bass_kernel_spmd

    nc = bacc.Bacc("TRN2", target_bir_lowering=False, num_devices=1)
    given = dict(x=L0_attn_x, w_down=L0_attn_Wc_down, w_q=L0_attn_Wq_up, w_kv=L0_attn_Wkv_up,
                 w_proj=L0_attn_Wc_proj, w_real=L0_ffn_w_freq_real, w_imag=L0_ffn_w_freq_imag,
                 bias=L0_ffn_bias, consts=constants())
    arrays, args = {}, []
    for name, a in given.items():
        a = np.ascontiguousarray(a)
        arrays[f"in_{name}"] = a
        args.append(nc.dram_tensor(f"in_{name}", a.shape, mybir.dt.from_np(a.dtype),
                                   kind="ExternalInput").ap())
    args.append(nc.dram_tensor("out", (B, T, D), mybir.dt.float32, kind="ExternalOutput").ap())
    macaron_program(nc, *args)
    r = run_bass_kernel_spmd(nc, [arrays], core_ids=[0])
    return r.results[0]["out"]
```

```python
from contextlib import ExitStack

import numpy as np

import concourse.bass as bass
from concourse import mybir

B, T, D = 4, 1024, 128
HEADS, HD, LATENT = 16, 8, 64
P = 128
BLK = 512
BLOCKS = B * T // BLK
TILES = BLK // P
GH = 4
GROUPS = HEADS // GH
UNITS = B * GROUPS
BODIES = UNITS // 2
PARTS = 3
ROWS = PARTS * PARTS * HD
ROWS_ALL = 96
NT = T // P
TAIL_S1 = 5
LEAD = 15
PRO_AHEAD, EPI_BEHIND = 3, 2
PAUSES = {"proj": 2, "ffn": 2, "q": 2, "kv": 1}
POST_TICKS, JOB_TICKS = 1, 2
EPS = 1e-5
RSQRT_BITS = float(0x5F3759DF)
SCALE = 1.0 / float(np.sqrt(HD))
HIDE = -1e38
C_ID, C_COS, C_SIN, C_NSIN, C_CAUSAL, C_ALL = 0, 128, 256, 384, 512, 640


def constants():
    c = np.zeros((P, C_ALL), np.float64)
    j = np.arange(P)
    turn = 2 * np.pi * (np.outer(j, j) % P) / P
    c[:, C_ID:C_ID + P] = np.eye(P)
    c[:, C_COS:C_COS + P] = np.cos(turn)
    c[:, C_SIN:C_SIN + P] = np.sin(turn)
    c[:, C_NSIN:C_NSIN + P] = -np.sin(turn)
    c[:, C_CAUSAL:C_CAUSAL + P] = np.where(j[:, None] > j[None, :], HIDE, 0.0)
    return c.astype(np.float32)


def sweep1_tiles():
    out = []
    for tb in range(NT):
        keys = P * (tb + 1)
        for lo in range(0, keys, 512):
            width = min(512, keys - lo)
            heads = min(512 // width, GH // 2 if tb == 0 else GH)
            out += [(tb, lo, width, h, heads, lo + width == keys) for h in range(0, GH, heads)]
    return out


S1 = sweep1_tiles()
N1 = len(S1)
S1_BANKS = 3
assert N1 % S1_BANKS == 0 and LEAD % S1_BANKS == 0


def s1_cost(tile):
    return 67 + tile[2] * tile[4] / 0.96


def groups_of(k):
    out = []
    for c in range(2):
        for i in range(4 * c + 4):
            first = max(0, P * i - 512 * c)
            out.append((k, c, i, 512 - first, first))
    return out


DVE_COST = {"ln1a": 2000, "ln1b": 600, "ln2b": 600, "ln3b": 600, "ffn": 3200, "proj": 3200, "ffn3": 600,
            "q": 1400, "kv": 1000, "sel": 600, "mT": 250, "max": 800}


def body_schedule(pro, epi, s1_units):
    s1 = [(u, n) for u, lo, hi in s1_units for n in range(lo, hi)]
    done = {n: u for n, (u, t) in enumerate(s1) if t == N1 - 1}
    groups = groups_of(0) + groups_of(1)
    jobs = [(5, "sel00"), (14, "sel01"), (18, "sel10")]
    dos = []
    if pro:
        dos += [(1, "ln1a"), (4, "ln1b"), (9, "ln2b")]
        jobs += [(5, "zT"), (6, "ffn"), (10, "z2T"), (11, "q"), (12, "kv"), (15, "kT")]
    if epi:
        dos += [(7, "ln3b")]
        jobs += [(3, "yT"), (5, "proj"), (8, "z3T"), (10, "ffn3")]
    jobs, dos = sorted(jobs), sorted(dos)

    def cost(name):
        return DVE_COST.get(name[:3] if name[:3] == "sel" else name[:2] if name[:2] == "mT" else name, 0)

    total = 2 * sum(s1_cost(t) for t in S1) + sum(cost(n) for _, n in jobs + dos) + 2 * (
        DVE_COST["max"] + DVE_COST["mT"])
    work = sum(g[3] for g in groups)
    out, at, n_s1, n_st, spent = [], 0, 0, 0, 0.0
    tail = TAIL_S1 if len(s1_units) > 1 else 0
    running, since, pause = None, 0, 0

    def emit(kind, name):
        nonlocal spent
        out.append((kind, name))
        if kind != "job":
            spent += cost(name)

    for s, g in enumerate(groups):
        w = g[3]
        per = 1 if w > 256 else 2
        tiles = [(s, n_st + n, n * per, per) for n in range(GH // per)]
        n_st += len(tiles)
        for n, t in enumerate(tiles):
            out.append(("st", g, t))
            since += 1
            if running and since >= POST_TICKS:
                emit("post", running)
                pause = PAUSES.get(running, 0)
                running, since = None, 0
            elif not running and since >= JOB_TICKS + pause and jobs and jobs[0][0] <= s:
                running, since = jobs.pop(0)[1], 0
                emit("job", running)
            upto = (at + w * (n + 1) / len(tiles)) / work * total
            while n_s1 < len(s1) - tail and spent < upto:
                out.append(("s1", n_s1, s1[n_s1]))
                spent += s1_cost(S1[s1[n_s1][1]])
                if n_s1 in done:
                    out.append(("max", done[n_s1]))
                    spent += DVE_COST["max"]
                    jobs.insert(0, (s, f"mT{done[n_s1]}"))
                    since, pause = min(since, JOB_TICKS - 3), 0
                n_s1 += 1
        at += w
        if s:
            out.append(("pv", s - 1, groups[s - 1]))
        while dos and dos[0][0] <= s:
            emit("do", dos.pop(0)[1])
    if running:
        emit("post", running)
    last = [("s1", n, s1[n]) for n in range(n_s1, len(s1))]
    assert not any(n in done for n in range(n_s1, len(s1))) and not jobs and not dos
    out += last[:1] + [("pv", len(groups) - 1, groups[-1])] + last[1:3]
    out += [("job", "sel11"), ("post", "sel11")] + last[3:]
    return out


def macaron_program(nc, x, w_down, w_q, w_kv, w_proj, w_real, w_imag, bias, consts, out):
    f32, bf16 = mybir.dt.float32, mybir.dt.bfloat16
    i32 = mybir.dt.int32
    ALU, ACT, AX = mybir.AluOpType, mybir.ActivationFunctionType, mybir.AxisListType
    x_blk = x.rearrange("b (h n p) c -> (b h) p n c", n=TILES, p=P)
    out_blk = out.rearrange("b (h n p) c -> (b h) p n c", n=TILES, p=P)

    def dram(name, shape, dt):
        return nc.dram_tensor(name, shape, dt, kind="Internal").ap()

    q_dram = dram("q_parts_dram", [B, GROUPS, PARTS, HD * GH, T], bf16)
    k_dram = dram("k_rows_dram", [B, PARTS, PARTS, HD, T], bf16)
    v_dram = dram("v_dram", [B, P, T // P, 32], f32)
    x1_dram = dram("x1_dram", [BLOCKS, P, TILES * D], f32)
    y_dram = dram("y_dram", [B, T, D], f32)
    y_blk = y_dram.rearrange("b (h n p) c -> (b h) p n c", n=TILES, p=P)

    ctx = ExitStack()
    with ctx:
        def sb(name, shape, dt=f32):
            return ctx.enter_context(nc.sbuf_tensor(name, shape, dt))

        def bank(name):
            return ctx.enter_context(nc.psum_tensor(name, [P, 512], f32))

        def sem(name):
            return ctx.enter_context(nc.semaphore(name))

        const = sb("const", [P, C_ALL])
        ident, cos, sin, nsin = (const[:, c:c + P] for c in (C_ID, C_COS, C_SIN, C_NSIN))
        ident16 = sb("ident16", [P, P], bf16)
        causal16 = sb("causal16", [P, P], bf16)
        wr, wi = sb("wr", [P, D]), sb("wi", [P, D])
        wd, wq, wkv = sb("wd", [P, LATENT]), sb("wq", [LATENT, D]), sb("wkv", [LATENT, 2 * HD])
        wp = sb("wp", [P, D])
        bias_half = sb("bias_half", [P, D])
        bias_in = sb("bias_in", [P, D])
        ab = sb("ab", [P, 2 * D])
        mask_in = sb("mask_in", [P, 2 * P])
        m_half = sb("m_half", [P, D])
        wdT = sb("wdT", [LATENT, P])
        w_dq, w_dkv = sb("w_dq", [P, D]), sb("w_dkv", [P, 2 * HD])
        q1 = sb("q1", [ROWS_ALL, 2, GH, T], bf16)
        q2 = sb("q2", [ROWS_ALL, 2, GH, T], bf16)
        k1 = sb("k1", [ROWS_ALL, 2, T], bf16)
        k2 = sb("k2", [ROWS_ALL, 2, T], bf16)
        v1 = sb("v1", [P, 2, T // P, 32])
        probs = sb("probs", [P, 3, GH, 512])
        o_sb = sb("o_sb", [P, 512])
        rec = sb("rec", [P, TILES, GH])
        y_sb = sb("y_sb", [P, 2, T // P, GH * HD])
        mx = sb("mx", [P, 2, GH, NT])
        mx_pair = sb("mx_pair", [P, 2, 2, GH, NT // 2])
        m_rest = sb("m_rest", [P, GH * NT])
        m_parts = sb("m_parts", [P, PARTS, GH * NT], bf16)
        mT = sb("mT", [PARTS * GH * NT, P], bf16)
        def twice(name, shape, dt=f32):
            return [sb(f"{name}{m}", shape, dt) for m in range(2)]

        x_sb, xb, x1, z1, z2 = (twice(n, [P, TILES, D]) for n in ("x_sb", "xb", "x1", "z1", "z2"))
        z1T, z2T = twice("z1T", [P, BLK]), twice("z2T", [P, BLK])
        q_parts, q_rest = twice("q_parts", [P, PARTS, BLK], bf16), twice("q_rest", [P, BLK])
        k_cols, k_rest = twice("k_cols", [P, TILES, PARTS, HD], bf16), twice("k_rest", [P, TILES, HD])
        k_parts = twice("k_parts", [PARTS * HD, BLK], bf16)
        v_out = twice("v_out", [P, TILES, 32])
        y_last = twice("y_last", [P, TILES, D])
        x1_in, x2, x2b, z3, out_sb = (
            twice(n, [P, TILES, D]) for n in ("x1_in", "x2", "x2b", "z3", "out_sb"))
        y_in = sb("y_in", [P, TILES, D])
        yT, z3T = twice("yT", [P, BLK]), twice("z3T", [P, BLK])
        stats, mv, rstd, var_eps, guess_bits, newton = {}, {}, {}, {}, {}, {}
        for n in (1, 2, 3):
            for m in range(2):
                stats[n, m], mv[n, m] = sb(f"stats{n}{m}", [P, TILES, 6]), sb(f"mv{n}{m}", [P, TILES, 2])
                rstd[n, m], var_eps[n, m] = sb(f"rstd{n}{m}", [P, TILES]), sb(f"var_eps{n}{m}", [P, TILES])
                guess_bits[n, m] = sb(f"guess_bits{n}{m}", [P, TILES], i32)
                newton[n, m] = sb(f"newton{n}{m}", [P, 2, TILES])
        cell = sb("cell", [P, 2])
        dve_dot, act_dot = sb("dve_dot", [1, 64]), sb("act_dot", [1, 64])
        st = [bank(f"st{n}") for n in range(3)]
        s1p = [bank(f"s1p{n}") for n in range(3)]
        o_ps = bank("o_ps")
        misc = bank("misc")
        misc_of = [misc, o_ps]

        (init_done, x1_ready, q_ready, k_ready, v_ready, pro_stored, out_ready, out_stored,
         y_ready, y_stored, mT_ready) = (sem(n) for n in (
             "init_done", "x1_ready", "q_ready", "k_ready", "v_ready", "pro_stored", "out_ready",
             "out_stored", "y_ready", "y_stored", "mT_ready"))
        w_loaded, wp_loaded, z_ready, m_ready, s1_free, kc_ready = (sem(n) for n in (
            "w_loaded", "wp_loaded", "z_ready", "m_ready", "s1_free", "kc_ready"))
        misc_free = [sem(f"misc_free{n}") for n in range(2)]
        s1_loaded = [sem(f"s1_loaded{n}") for n in range(2)]
        s2_loaded = [sem(f"s2_loaded{n}") for n in range(2)]
        exp_done, o_taken = sem("exp_done"), sem("o_taken")
        misc_act, st_ready, pv_done, act_start, act_chain = (sem(n) for n in (
            "misc_act", "st_ready", "pv_done", "act_start", "act_chain"))
        misc_dve, s1_ready, xb_ready, x2b_ready, q1_ready, chain = (
            sem(n) for n in ("misc_dve", "s1_ready", "xb_ready",
                             "x2b_ready", "q1_ready", "chain"))
        dve_start, bias_loaded = sem("dve_start"), sem("bias_loaded")
        x_loaded = [sem(f"x_loaded{n}") for n in range(2)]
        x1_loaded = [sem(f"x1_loaded{n}") for n in range(2)]
        y_loaded = sem("y_loaded")
        x_seen, x2_seen, q2_ready = (sem(n) for n in ("x_seen", "x2_seen", "q2_ready"))
        mv_ready, rstd_ready, pool_chain = sem("mv_ready"), sem("rstd_ready"), sem("pool_chain")

        block = ctx.enter_context(nc.Block())

        def counter():
            counts = {}

            def seen(s, n=1):
                key = s.name
                counts[key] = (s, counts.get(key, (s, 0))[1] + n)
                return counts[key][1]

            def settle(eng):
                for s, n in counts.values():
                    eng.sem_inc(s, -n)
                counts.clear()
            return seen, settle

        BODY_KINDS = [
            (0, 2, True, False, [(1, LEAD, N1), (2, 0, N1), (3, 0, LEAD)], 2),
            (2, 5, True, True, [(1, LEAD, N1), (2, 0, N1), (3, 0, LEAD)], 2),
            (5, 6, False, True, [(1, LEAD, N1), (2, 0, N1), (3, 0, LEAD)], 2),
            (6, 7, False, True, [(1, LEAD, N1), (2, 0, N1), (3, 0, LEAD)], 1),
            (7, 8, False, True, [(1, LEAD, N1)], 0),
        ]

        def run_bodies(eng, body):
            for first, end, pro, epi, s1_units, loads in BODY_KINDS:
                schedule = body_schedule(pro, epi, s1_units)
                if end - first > 1:
                    with eng.Fori(first, end) as i:
                        body(i, pro, epi, schedule, loads)
                else:
                    body(first, pro, epi, schedule, loads)

        def ahead_schedule():
            out = [("do", "ln1a"), ("do", "ln1b"), ("job", "zT"), ("post", "zT"), ("job", "ffn"), ("post", "ffn")]
            todo = [("do", "ln2b")]
            for name in ("z2T", "q", "kv", "kT"):
                todo += [("job", name), ("post", name)]
            tiles = [(0, n) for n in range(N1)] + [(1, n) for n in range(LEAD)]
            for n, (u, t) in enumerate(tiles):
                out.append(("s1", n, (u, t)))
                if n == N1 - 1:
                    out += [("max", 0)]
                if n == N1 + 4:
                    out += [("job", "mT0"), ("post", "mT0")]
                if n % 4 == 3 and todo:
                    out.append(todo.pop(0))
            return out + todo

        PRO_PAIR = ["ln1a", "ln1b", "zT", "ffn", "ln2b", "z2T", "q", "kv", "kT"]
        EPI_PAIR = ["y_lastT", "proj", "ln3b", "z3T", "ffn3"]
        JOBS = {"zT", "ffn", "z2T", "q", "kv", "kT", "y_lastT", "proj", "z3T", "ffn3"}

        @block.sync
        def _(sp):
            seen, settle = counter()

            def load_x(j, m=0):
                sp.dma_start(x_sb[m][:, :, :], x_blk[bass.ds(j, 1)].rearrange("o p n c -> p (o n) c")
                             ).then_inc(x_loaded[m], 16)

            def store_x1(j, m=0):
                sp.wait_ge(x1_ready, seen(x1_ready))
                sp.dma_start(x1_dram[bass.ds(j, 1)].rearrange("o p f -> (o p) f"),
                             x1[m][:, :, :].rearrange("p n c -> p (n c)")).then_inc(pro_stored, 16)

            def store_q(j, m=0):
                sp.wait_ge(q_ready, seen(q_ready))
                for a in range(PARTS):
                    sp.dma_start(
                        q_dram[bass.ds(j // 2, 1), :, a, :, bass.ds((j % 2) * BLK, BLK)]
                        .rearrange("o g r t -> (o g) r t"), q_parts[m][:, a, :]).then_inc(pro_stored, 16)

            def store_k(j, m=0):
                sp.wait_ge(k_ready, seen(k_ready))
                for a in range(PARTS):
                    sp.dma_start(k_dram[bass.ds(j // 2, 1), :, a, :, bass.ds((j % 2) * BLK, BLK)]
                                 .rearrange("o b r t -> (o b) r t"), k_parts[m][:, :]).then_inc(pro_stored, 16)

            def store_v(j, m=0):
                sp.wait_ge(v_ready, seen(v_ready))
                sp.dma_start(v_dram[bass.ds(j // 2, 1), :, bass.ds((j % 2) * TILES, TILES), :]
                             .rearrange("o p n c -> (o p) n c"), v_out[m][:, :, :]).then_inc(pro_stored, 16)

            def load_q(dst, half, m, done):
                src = q_dram[bass.ds(half // 2, 1), bass.ds((half % 2) * 2 + m, 1)]
                sp.dma_start(dst[0:ROWS, m, :, :].rearrange("p h t -> p (h t)"),
                             src.rearrange("o g a (d h) t -> (o g a d) (h t)", h=GH).unsqueeze(0)
                             .broadcast_to([PARTS, PARTS * HD, GH * T])).then_inc(done, 16)

            def load_k(dst, m, half, done):
                sp.dma_start(dst[0:ROWS, m, :],
                             k_dram[bass.ds(half // 2, 1)].rearrange("o b a r t -> (o b a r) t")
                             ).then_inc(done, 16)

            def load_sweep1(half, m):
                load_q(q1, half, m, s1_loaded[m])
                load_k(k1, m, half, s1_loaded[m])

            def load_sweep2(half, m):
                load_q(q2, half, m, s2_loaded[m])
                load_k(k2, m, half, s2_loaded[m])
                load_v(half, m)

            def load_v(half, m):
                sp.dma_start(v1[:, m, :, :].rearrange("p n c -> p (n c)"),
                             v_dram[bass.ds(half // 2, 1)].rearrange("o p n c -> (o p) (n c)")
                             ).then_inc(s2_loaded[m], 16)

            def max_rows(m):
                sp.wait_ge(mT_ready, seen(mT_ready))
                sp.dma_start(q2[ROWS:ROWS + PARTS, m, :, :].rearrange("a h t -> a (h t)"), mT[:, :]
                             ).then_inc(s2_loaded[m], 16)

            def store_y(half, m):
                sp.dma_start(
                    y_dram[bass.ds(half // 2, 1), :, bass.ds((half % 2) * 64 + 32 * m, 32)]
                    .rearrange("o (n p) c -> p (o n) c", p=P), y_sb[:, m, :, :]).then_inc(y_stored, 16)

            def load_y(j):
                sp.dma_start(y_in[:, :, :], y_blk[bass.ds(j, 1)].rearrange("o p n c -> p (o n) c")
                             ).then_inc(y_loaded, 16)

            def load_x1(j, m=0):
                sp.dma_start(x1_in[m][:, :, :].rearrange("p n c -> p (n c)"),
                             x1_dram[bass.ds(j, 1)].rearrange("o p f -> (o p) f")).then_inc(x1_loaded[m], 16)

            def store_out(j, m=0):
                sp.wait_ge(out_ready, seen(out_ready))
                sp.dma_start(out_blk[bass.ds(j, 1)].rearrange("o p n c -> p (o n) c"), out_sb[m][:, :, :]
                             ).then_inc(out_stored, 16)

            load_x(0, 0)
            sp.dma_start(bias_in[:, :], bias.unsqueeze(0).broadcast_to([P, D])).then_inc(bias_loaded, 16)
            load_x(1, 1)
            for dst, src in ((wr[:, :], w_real), (wi[:, :], w_imag), (const[:, :], consts),
                             (wd[:, :], w_down), (wq[:, :], w_q), (wkv[:, :], w_kv)):
                sp.dma_start(dst, src).then_inc(w_loaded, 16)
            sp.dma_start(cell[:, :], consts[:, 0:2]).then_inc(act_start, 16)
            sp.dma_start(mask_in[:, 0:P], consts[:, C_ID:C_ID + P]).then_inc(dve_start, 16)
            sp.dma_start(mask_in[:, P:2 * P], consts[:, C_CAUSAL:C_CAUSAL + P]).then_inc(dve_start, 16)
            sp.dma_start(wp[:, :], w_proj).then_inc(wp_loaded, 16)
            for m in range(2):
                store_x1(m, m)
            load_x(2)
            for m in range(2):
                store_q(m, m)
            sp.wait_ge(init_done, seen(init_done, 2))
            for m in range(2):
                store_k(m, m)
            for m in range(2):
                store_v(m, m)
            sp.wait_ge(pro_stored, seen(pro_stored, 2 * 8 * 16))
            load_q(q1, 0, 0, s1_loaded[0])
            load_k(k1, 0, 0, s1_loaded[0])
            load_q(q1, 0, 1, s1_loaded[1])
            load_k(k1, 1, 0, s1_loaded[1])
            for m in range(2):
                load_q(q2, 0, m, s2_loaded[m])
                load_k(k2, m, 0, s2_loaded[m])
            for m in range(2):
                load_v(0, m)
            store_x1(2)
            max_rows(0)
            load_sweep1(1, 0)
            store_q(2)
            store_v(2)
            store_k(2)
            sp.wait_ge(pro_stored, seen(pro_stored, 128))
            settle(sp)

            def body(i, pro, epi, schedule, loads):
                to_dram = loads >= 2
                if epi:
                    load_y(i - EPI_BEHIND)
                    load_x1(i - EPI_BEHIND)
                if pro:
                    load_x(i + PRO_AHEAD)
                max_rows(1)
                if loads >= 1:
                    load_sweep1(i + 1, 1)
                if pro:
                    store_x1(i + PRO_AHEAD)
                if epi:
                    store_out(i - EPI_BEHIND)
                if loads == 0:
                    for m in range(2):
                        load_x1(BLOCKS - 2 + m, m)
                if pro:
                    store_q(i + PRO_AHEAD)
                sp.wait_ge(y_ready, seen(y_ready))
                if to_dram:
                    store_y(i, 0)
                if loads >= 1:
                    load_sweep2(i + 1, 0)
                if pro:
                    store_v(i + PRO_AHEAD)
                    store_k(i + PRO_AHEAD)
                if to_dram:
                    sp.wait_ge(y_stored, seen(y_stored, 16))
                if loads >= 1:
                    max_rows(0)
                if pro:
                    sp.wait_ge(pro_stored, seen(pro_stored, 128))
                if loads >= 2:
                    load_sweep1(i + 2, 0)
                if epi:
                    sp.wait_ge(out_stored, seen(out_stored, 16))
                sp.wait_ge(y_ready, seen(y_ready))
                if to_dram:
                    store_y(i, 1)
                if loads >= 1:
                    load_sweep2(i + 1, 1)
                if to_dram:
                    sp.wait_ge(y_stored, seen(y_stored, 16))
                settle(sp)

            run_bodies(sp, body)
            for m in range(2):
                store_out(BLOCKS - 2 + m, m)
            sp.wait_ge(out_stored, seen(out_stored, 32))

        @block.tensor
        def _(pe):
            seen, settle = counter()
            mm = nc.tensor.matmul
            pe.wait_ge(w_loaded, seen(w_loaded, 6 * 16))
            mm(misc[:, 0:P], wr[:, :], cos, start=True, stop=False)
            mm(misc[:, 0:P], wi[:, :], sin, start=False, stop=True)
            mm(misc[:, P:2 * P], wi[:, :], cos, start=True, stop=False)
            mm(misc[:, P:2 * P], wr[:, :], nsin, start=False, stop=True)
            nc.tensor.transpose(misc[0:LATENT, 2 * P:3 * P], wd[:, :], ident).then_inc(misc_dve, 1)
            pe.wait_ge(misc_free[0], seen(misc_free[0]))
            mm(misc[:, 0:P], ab[:, 0:P], cos, start=True, stop=False)
            mm(misc[:, 0:P], ab[:, P:2 * P], nsin, start=False, stop=True)
            mm(misc[:, P:2 * P], wdT[:, :], wq[:, :], start=True, stop=True)
            mm(misc[:, 2 * P:2 * P + 2 * HD], wdT[:, :], wkv[:, :], start=True, stop=True
               ).then_inc(misc_dve, 1)
            pe.wait_ge(misc_free[0], seen(misc_free[0]))
            settle(pe)

            def transposes(src, m, done):
                for n in range(TILES):
                    last = nc.tensor.transpose(misc_of[m][:, n * P:(n + 1) * P], src[:, n, :], ident)
                last.then_inc(done, 1)

            def by_tile(lhs, rhs, width, m, done):
                for n in range(TILES):
                    last = mm(misc_of[m][:, n * width:(n + 1) * width], lhs[:, n * P:(n + 1) * P], rhs,
                              start=True, stop=True)
                last.then_inc(done, 1)

            in_use = [False, False]

            def free(m=0):
                if in_use[m]:
                    pe.wait_ge(misc_free[m], seen(misc_free[m]))
                in_use[m] = False

            def job(name, m=0):
                free(m)
                in_use[m] = True
                if name in ("zT", "z2T", "z3T"):
                    pe.wait_ge(z_ready, seen(z_ready))
                    transposes({"zT": z1, "z2T": z2, "z3T": z3}[name][m], m, misc_act)
                elif name == "yT":
                    pe.wait_ge(y_loaded, seen(y_loaded, 16))
                    transposes(y_in, m, misc_act)
                elif name == "y_lastT":
                    transposes(y_last[m], m, misc_act)
                elif name == "ffn":
                    by_tile(z1T[m], m_half[:, :], D, m, misc_dve)
                elif name == "ffn3":
                    by_tile(z3T[m], m_half[:, :], D, m, misc_dve)
                elif name == "proj":
                    by_tile(yT[m], wp[:, :], D, m, misc_dve)
                elif name == "q":
                    mm(misc_of[m][:, :], w_dq[:, :], z2T[m][:, :], start=True, stop=True
                       ).then_inc(misc_act, 1)
                elif name == "kv":
                    by_tile(z2T[m], w_dkv[:, :], 2 * HD, m, misc_act)
                elif name == "kT":
                    pe.wait_ge(kc_ready, seen(kc_ready))
                    for n in range(TILES):
                        last = nc.tensor.transpose(
                            misc_of[m][:, :].bitcast(bf16)[0:PARTS * HD, n * P:(n + 1) * P],
                            k_cols[m][:, n, :, :].rearrange("p a d -> p (a d)"), ident16[:, :])
                    last.then_inc(misc_act, 1)
                elif name[:2] == "mT":
                    pe.wait_ge(m_ready, seen(m_ready))
                    nc.tensor.transpose(misc[:, 0:64].bitcast(bf16)[0:PARTS * GH * NT, :],
                                        m_parts[:, :, :].rearrange("p a n -> p (a n)"), ident16[:, :]
                                        ).then_inc(misc_dve, 1)
                elif name[:3] == "sel":
                    pe.wait_ge(o_taken, seen(o_taken))
                    for n in range(TILES):
                        last = nc.tensor.transpose(misc[:, n * P:(n + 1) * P],
                                                   o_sb[:, n * P:(n + 1) * P], ident)
                    last.then_inc(misc_dve, 1)

            def sweep1(n, u, t):
                tb, lo, width, h0, heads, diagonal = S1[t]
                m = u % 2
                if t == 0:
                    pe.wait_ge(s1_loaded[m], seen(s1_loaded[m], 32))
                pe.wait_ge(s1_free, seen(s1_free))
                ps = s1p[n % 3]
                for e in range(heads):
                    last = mm(ps[:, e * width:(e + 1) * width], q1[:, m, h0 + e, P * tb:P * tb + P],
                              k1[:, m, lo:lo + width], start=True, stop=not diagonal)
                    if diagonal:
                        last = mm(ps[:, (e + 1) * width - P:(e + 1) * width], causal16[:, :],
                                  ident16[:, :], start=False, stop=True)
                last.then_inc(s1_ready, 1)

            def in_pairs(names):
                for name in names:
                    for m in range(2):
                        if name in JOBS:
                            job(name, m)
                free(0)
                free(1)
                settle(pe)

            in_pairs(PRO_PAIR)
            pe.wait_ge(wp_loaded, 16)
            pe.sem_inc(s1_free, 3)
            for item in ahead_schedule():
                if item[0] == "s1":
                    sweep1(item[1], *item[2])
                elif item[0] == "job":
                    job(item[1])
            settle(pe)

            def body(i, pro, epi, schedule, loads):
                group_of = [item[2][0] for item in schedule if item[0] == "st"]
                exps = 0

                for item in schedule:
                    if item[0] == "st":
                        _, (k, c, ki, w, first), (s, n, h0, per) = item
                        if c == 0 and ki == 0 and h0 == 0:
                            pe.wait_ge(s2_loaded[k], seen(s2_loaded[k], 64))
                        if n - 2 > exps:
                            pe.wait_ge(exp_done, seen(exp_done, n - 2 - exps))
                            exps = n - 2
                        for e in range(per):
                            last = mm(st[n % 3][:, e * w:(e + 1) * w], k2[:, k, P * ki:P * ki + P],
                                      q2[:, k, h0 + e, 512 * c + first:512 * c + 512],
                                      start=True, stop=ki < 4 * c)
                            if ki >= 4 * c:
                                last = mm(st[n % 3][:, e * w:e * w + P], ident16[:, :], causal16[:, :],
                                          start=False, stop=True)
                        last.then_inc(st_ready, 1)
                    elif item[0] == "s1":
                        sweep1(item[1], *item[2])
                    elif item[0] == "pv":
                        _, s, (k, c, ki, w, first) = item
                        upto = sum(g <= s for g in group_of)
                        if upto > exps:
                            pe.wait_ge(exp_done, seen(exp_done, upto - exps))
                            exps = upto
                        for h in range(GH):
                            last = mm(o_ps[32 * h:32 * h + 32, first:512], v1[:, k, ki, :],
                                      probs[:, s % 3, h, 0:w], start=(ki == 0), stop=(ki == 4 * c + 3))
                        last.then_inc(pv_done, 1)
                    elif item[0] == "job":
                        job(item[1])
                settle(pe)

            run_bodies(pe, body)
            in_pairs(EPI_PAIR)

        @block.scalar
        def _(act):
            seen, settle = counter()
            copy = nc.scalar.copy
            act.wait_ge(act_start, seen(act_start, 16))
            dots = [0]

            def dot(s):
                dots[0] = (dots[0] + 1) % 64
                copy(act_dot[:, dots[0]:dots[0] + 1], cell[0:1, 0:1]).then_inc(s, 1)

            def zeros(t):
                copy(t[64:96, :, :, :].rearrange("p m h t -> p (m h t)"),
                     cell[64:96, 0:1].broadcast_to([32, 2 * GH * T])).then_inc(act_chain, 1)
                act.wait_ge(act_chain, seen(act_chain))

            zeros(q2)

            def post(name, m=0):
                bank_ = misc_of[m]
                if name in ("zT", "z2T", "z3T", "yT", "y_lastT"):
                    act.wait_ge(misc_act, seen(misc_act))
                    dst = {"zT": z1T, "z2T": z2T, "z3T": z3T, "yT": yT, "y_lastT": yT}[name][m]
                    copy(dst[:, :], bank_[:, :]).then_inc(misc_free[m], 1)
                elif name == "q":
                    act.wait_ge(misc_act, seen(misc_act))
                    copy(q_parts[m][:, 0, :], bank_[:, :]).then_inc(q1_ready, 1)
                elif name == "kv":
                    act.wait_ge(misc_act, seen(misc_act))
                    copy(v_out[m][:, :, 0:HD],
                         bank_[:, 0:TILES * 2 * HD].rearrange("p (n c) -> p n c", c=2 * HD)[:, :, HD:]
                         ).then_inc(q1_ready, 1)
                    dot(v_ready)
                elif name == "kT":
                    act.wait_ge(misc_act, seen(misc_act))
                    copy(k_parts[m][:, :], bank_[:, :].bitcast(bf16)[0:PARTS * HD, 0:BLK]
                         ).then_inc(misc_free[m], 1)
                    dot(k_ready)

            for name in PRO_PAIR:
                for m in range(2):
                    post(name, m)
                if name == "zT":
                    zeros(q1)
                    dot(init_done)
            for item in ahead_schedule():
                if item[0] == "post":
                    post(item[1])
            settle(act)
            act.sem_inc(pv_done, 3)

            def body(i, pro, epi, schedule, loads):
                for item in schedule:
                    if item[0] == "st":
                        _, (k, c, ki, w, first), (s, n, h0, per) = item
                        if h0 == 0:
                            act.wait_ge(pv_done, s + 1)
                        act.wait_ge(st_ready, seen(st_ready))
                        nc.scalar.activation(
                            probs[:, s % 3, h0:h0 + per, 0:w],
                            st[n % 3][:, 0:per * w].rearrange("p (e w) -> p e w", e=per),
                            ACT.Exp, scale=SCALE).then_inc(exp_done, 1)
                    elif item[0] == "pv":
                        _, s, (k, c, ki, w, first) = item
                        if ki == 4 * c + 3:
                            act.wait_ge(pv_done, s + 4)
                            copy(o_sb[:, :], o_ps[:, :]).then_inc(o_taken, 1)
                    elif item[0] == "post":
                        post(item[1])
                seen(pv_done, 24)
                settle(act)

            run_bodies(act, body)
            for name in EPI_PAIR:
                for m in range(2):
                    post(name, m)

        @block.vector
        def _(dve):
            seen, settle = counter()
            v = nc.vector

            def linked(ins):
                ins.then_inc(chain, 1)
                dve.wait_ge(chain, seen(chain))

            dots = [0]

            def dot(s):
                dots[0] = (dots[0] + 1) % 64
                v.memset(dve_dot[:, dots[0]:dots[0] + 1], 0.0).then_inc(s, 1)

            def statistics(src, ln, first_done, second_done):
                for n in range(TILES):
                    ins = v.bn_stats(stats[ln][:, n, :], src[:, n, :])
                    if n == 0 and first_done is not None:
                        ins.then_inc(first_done, 1)
                    if n == 1 and second_done is not None:
                        ins.then_inc(second_done, 1)
                linked(ins)
                for n in range(TILES):
                    ins = v.bn_aggr(mv[ln][:, n, :], stats[ln][:, n, :])
                linked(ins)
                linked(v.tensor_scalar(var_eps[ln][:, :], mv[ln][:, :, 1], EPS, None, ALU.add))
                linked(v.tensor_scalar(guess_bits[ln][:, :], var_eps[ln][:, :].bitcast(i32), 1, None,
                                       ALU.logical_shift_right))
                v.tensor_scalar(rstd[ln][:, :].bitcast(i32), guess_bits[ln][:, :], -1.0, RSQRT_BITS,
                                ALU.mult, ALU.add).then_inc(mv_ready, 1)

            def normalise(src, dst, ln):
                dve.wait_ge(rstd_ready, seen(rstd_ready))
                for n in range(TILES):
                    ins = v.tensor_scalar(dst[:, n, :], src[:, n, :], mv[ln][:, n, 0:1],
                                          rstd[ln][:, n:n + 1], ALU.subtract, ALU.mult)
                ins.then_inc(z_ready, 1)

            def flat(t):
                return t[:, :, :].rearrange("p n c -> p (n c)")

            def do(name, m=0):
                if name == "ln1a":
                    dve.wait_ge(x_loaded[m], seen(x_loaded[m], 16))
                    statistics(x_sb[m], (1, m), x_seen, None)
                elif name == "ln1b":
                    normalise(x_sb[m], z1[m], (1, m))
                elif name == "ln2b":
                    normalise(x1[m], z2[m], (2, m))
                elif name == "ln3b":
                    normalise(x2[m], z3[m], (3, m))

            def post(name, m=0, last_body=None):
                bank_ = misc_of[m]
                if name == "ffn":
                    dve.wait_ge(xb_ready, seen(xb_ready))
                    dve.wait_ge(misc_dve, seen(misc_dve))
                    linked(v.tensor_tensor(flat(x1[m]), bank_[:, :], flat(xb[m]), ALU.add))
                    statistics(x1[m], (2, m), misc_free[m], x1_ready)
                elif name == "q":
                    dve.wait_ge(q1_ready, seen(q1_ready))
                    linked(v.tensor_tensor(q_rest[m][:, :], bank_[:, :], q_parts[m][:, 0, :], ALU.subtract))
                    v.tensor_copy(q_parts[m][:, 1, :], q_rest[m][:, :]).then_inc(q2_ready, 1)
                    dot(misc_free[m])
                elif name == "kv":
                    dve.wait_ge(q1_ready, seen(q1_ready))
                    k_ps = bank_[:, 0:TILES * 2 * HD].rearrange("p (n c) -> p n c", c=2 * HD)[:, :, 0:HD]
                    linked(v.tensor_copy(k_cols[m][:, :, 0, :], k_ps))
                    linked(v.tensor_tensor(k_rest[m][:, :, :], k_ps, k_cols[m][:, :, 0, :], ALU.subtract))
                    dot(misc_free[m])
                    linked(v.tensor_copy(k_cols[m][:, :, 1, :], k_rest[m][:, :, :]))
                    v.tensor_tensor(k_cols[m][:, :, 2, :], k_rest[m][:, :, :], k_cols[m][:, :, 1, :],
                                    ALU.subtract).then_inc(kc_ready, 1)
                elif name == "proj":
                    dve.wait_ge(x1_loaded[m], seen(x1_loaded[m], 16))
                    dve.wait_ge(misc_dve, seen(misc_dve))
                    linked(v.tensor_tensor(flat(x2[m]), bank_[:, :], flat(x1_in[m]), ALU.add))
                    statistics(x2[m], (3, m), misc_free[m], x2_seen)
                elif name == "ffn3":
                    dve.wait_ge(x2b_ready, seen(x2b_ready))
                    dve.wait_ge(misc_dve, seen(misc_dve))
                    v.tensor_tensor(flat(out_sb[m]), bank_[:, :], flat(x2b[m]), ALU.add
                                    ).then_inc(misc_free[m], 1)
                    dot(out_ready)
                elif name[:2] == "mT":
                    dve.wait_ge(misc_dve, seen(misc_dve))
                    v.tensor_copy(mT[:, :], misc[:, 0:64].bitcast(bf16)[0:PARTS * GH * NT, :]
                                  ).then_inc(misc_free[m], 1)
                    dot(mT_ready)
                elif name[:3] == "sel":
                    k, c = int(name[3]), int(name[4])
                    dve.wait_ge(misc_dve, seen(misc_dve))
                    sums = misc[:, :].rearrange("p (n h e) -> p n h e", n=TILES, h=GH)
                    linked(v.reciprocal(rec[:, :, :], sums[:, :, :, HD]))
                    dst = y_sb[:, k, TILES * c:TILES * c + TILES, :]
                    if last_body is not None:
                        group = 2 * (last_body % 2) + k
                        dst = y_last[c][:, :, GH * HD * group:GH * HD * (group + 1)]
                    v.tensor_tensor(
                        dst.rearrange("p n (h d) -> p n h d", h=GH),
                        sums[:, :, :, 0:HD], rec[:, :, :].unsqueeze(3).broadcast_to([P, TILES, GH, HD]),
                        ALU.mult).then_inc(misc_free[m], 1)
                    if c == 1:
                        dot(y_ready)

            def sweep1_max(n, u, t):
                tb, lo, width, h0, heads, diagonal = S1[t]
                dst = mx[:, u % 2, h0:h0 + heads, tb] if tb < NT // 2 else (
                    mx_pair[:, u % 2, lo // 512, h0:h0 + heads, tb - NT // 2])
                dve.wait_ge(s1_ready, seen(s1_ready))
                v.tensor_reduce(dst, s1p[n % 3][:, 0:heads * width].rearrange("p (e w) -> p e w", e=heads),
                                axis=AX.X, op=ALU.max).then_inc(s1_free, 1)

            def max_parts(u):
                m = u % 2
                dot(chain)
                dve.wait_ge(chain, seen(chain))
                linked(v.tensor_tensor(mx[:, m, :, NT // 2:], mx_pair[:, m, 0, :, :],
                                       mx_pair[:, m, 1, :, :], ALU.max))
                largest = mx[:, m, :, :].rearrange("p h n -> p (h n)")
                linked(v.tensor_scalar(m_parts[:, 0, :], largest, -1.0, None, ALU.mult))
                linked(v.scalar_tensor_tensor(m_rest[:, :], largest, -1.0, m_parts[:, 0, :],
                                              ALU.mult, ALU.subtract))
                linked(v.tensor_copy(m_parts[:, 1, :], m_rest[:, :]))
                v.tensor_tensor(m_parts[:, 2, :], m_rest[:, :], m_parts[:, 1, :], ALU.subtract
                                ).then_inc(m_ready, 1)

            def take(item, last_body=None):
                if item[0] == "s1":
                    sweep1_max(item[1], *item[2])
                elif item[0] == "max":
                    max_parts(item[1])
                elif item[0] == "do":
                    do(item[1])
                elif item[0] == "post":
                    post(item[1], last_body=last_body)

            dve.wait_ge(bias_loaded, seen(bias_loaded, 16))
            linked(v.tensor_scalar(bias_half[:, :], bias_in[:, :], 0.5, None, ALU.mult))
            for m in range(2):
                do("ln1a", m)
            v.memset(v_out[0][:, :, :], 0.0)
            linked(v.memset(v_out[1][:, :, :], 0.0))
            v.memset(v_out[0][:, :, HD:HD + 1], 1.0)
            v.memset(v_out[1][:, :, HD:HD + 1], 1.0)
            dve.wait_ge(misc_dve, seen(misc_dve))
            v.tensor_copy(ab[:, :], misc[:, 0:2 * P])
            v.tensor_copy(wdT[:, :], misc[0:LATENT, 2 * P:3 * P]).then_inc(misc_free[0], 1)
            for m in range(2):
                do("ln1b", m)
            dve.wait_ge(misc_dve, seen(misc_dve))
            v.tensor_scalar(m_half[:, :], misc[:, 0:P], 0.5 / D, None, ALU.mult)
            v.tensor_copy(w_dq[:, :].rearrange("p (g d h) -> p g d h", g=GROUPS, d=HD),
                          misc[:, P:2 * P].rearrange("p (g h d) -> p g d h", g=GROUPS, d=HD))
            v.tensor_copy(w_dkv[:, :], misc[:, 2 * P:2 * P + 2 * HD]).then_inc(misc_free[0], 1)
            v.memset(k1[64:96, :, :], 0.0)
            v.memset(k2[64:96, :, :], 1.0)
            dve.wait_ge(dve_start, seen(dve_start, 32))
            v.tensor_copy(ident16[:, :], mask_in[:, 0:P])
            linked(v.tensor_copy(causal16[:, :], mask_in[:, P:2 * P]))
            dot(init_done)
            for name in PRO_PAIR[2:]:
                for m in range(2):
                    do(name, m)
                    post(name, m)
            for item in ahead_schedule():
                take(item)
            settle(dve)

            def body(i, pro, epi, schedule, loads):
                for item in schedule:
                    take(item, i if loads < 2 else None)
                settle(dve)

            run_bodies(dve, body)
            for name in EPI_PAIR:
                for m in range(2):
                    do(name, m)
                    post(name, m)

        @block.gpsimd
        def _(pool):
            seen, settle = counter()
            g = nc.gpsimd

            def flat(t):
                return t[:, :, :].rearrange("p n c -> p (n c)")

            def with_bias(dst, src, ready):
                g.tensor_tensor(dst[:, :, :], src[:, :, :],
                                bias_half[:, :].unsqueeze(1).broadcast_to([P, TILES, D]), ALU.add
                                ).then_inc(ready, 1)

            def inverse_deviation(ln):
                pool.wait_ge(mv_ready, seen(mv_ready))
                a, b = newton[ln][:, 0, :], newton[ln][:, 1, :]
                for n in range(3):
                    if n:
                        pool.wait_ge(pool_chain, seen(pool_chain))
                    g.tensor_tensor(a, rstd[ln][:, :], rstd[ln][:, :], ALU.mult).then_inc(pool_chain, 1)
                    pool.wait_ge(pool_chain, seen(pool_chain))
                    g.tensor_tensor(b, a, var_eps[ln][:, :], ALU.mult).then_inc(pool_chain, 1)
                    pool.wait_ge(pool_chain, seen(pool_chain))
                    g.tensor_scalar(a, b, -0.5, 1.5, ALU.mult, ALU.add).then_inc(pool_chain, 1)
                    pool.wait_ge(pool_chain, seen(pool_chain))
                    g.tensor_tensor(rstd[ln][:, :], rstd[ln][:, :], a, ALU.mult
                                    ).then_inc(rstd_ready if n == 2 else pool_chain, 1)

            def work(name, m=0):
                if name == "ln1a":
                    pool.wait_ge(x_seen, seen(x_seen))
                    with_bias(xb[m], x_sb[m], xb_ready)
                    inverse_deviation((1, m))
                elif name == "ffn":
                    inverse_deviation((2, m))
                elif name == "q":
                    pool.wait_ge(q2_ready, seen(q2_ready))
                    g.tensor_tensor(q_parts[m][:, 2, :], q_rest[m][:, :], q_parts[m][:, 1, :], ALU.subtract
                                    ).then_inc(q_ready, 1)
                elif name == "proj":
                    pool.wait_ge(x2_seen, seen(x2_seen))
                    with_bias(x2b[m], x2[m], x2b_ready)
                    inverse_deviation((3, m))

            for name in PRO_PAIR:
                for m in range(2):
                    work(name, m)
            for item in ahead_schedule():
                if item[0] in ("do", "post"):
                    work(item[1])
            settle(pool)

            def body(i, pro, epi, schedule, loads):
                for item in schedule:
                    if item[0] in ("do", "post"):
                        work(item[1])
                settle(pool)

            run_bodies(pool, body)
            for name in EPI_PAIR:
                for m in range(2):
                    work(name, m)


def kernel(L0_attn_x, L0_attn_Wc_down, L0_attn_Wq_up, L0_attn_Wkv_up, L0_attn_Wc_proj,
           L0_ffn_w_freq_real, L0_ffn_w_freq_imag, L0_ffn_bias):
    import concourse.bacc as bacc
    from concourse.bass_utils import run_bass_kernel_spmd

    nc = bacc.Bacc("TRN2", target_bir_lowering=False, num_devices=1)
    given = dict(x=L0_attn_x, w_down=L0_attn_Wc_down, w_q=L0_attn_Wq_up, w_kv=L0_attn_Wkv_up,
                 w_proj=L0_attn_Wc_proj, w_real=L0_ffn_w_freq_real, w_imag=L0_ffn_w_freq_imag,
                 bias=L0_ffn_bias, consts=constants())
    arrays, args = {}, []
    for name, a in given.items():
        a = np.ascontiguousarray(a)
        arrays[f"in_{name}"] = a
        args.append(nc.dram_tensor(f"in_{name}", a.shape, mybir.dt.from_np(a.dtype),
                                   kind="ExternalInput").ap())
    args.append(nc.dram_tensor("out", (B, T, D), mybir.dt.float32, kind="ExternalOutput").ap())
    macaron_program(nc, *args)
    r = run_bass_kernel_spmd(nc, [arrays], core_ids=[0])
    return r.results[0]["out"]
```
